# Optimizing a Trainium2 kernel written in Bass

```python
import numpy as np
import jax
import jax.numpy as jnp

def _softmax(x, axis=-1):
    return jax.nn.softmax(x, axis=axis)

def _gelu(x):
    return jax.nn.gelu(x, approximate=True)

def _silu(x):
    return jax.nn.silu(x)

def _sigmoid(x):
    return jax.nn.sigmoid(x)

def _layernorm(x, axis=-1, eps=1e-05):
    m = jnp.mean(x, axis=axis, keepdims=True)
    v = jnp.var(x, axis=axis, keepdims=True)
    return (x - m) / jnp.sqrt(v + eps)

def _scatter_add(tgt, idx, src, axis=0):
    return tgt.at[idx].add(src)

def _segment_sum(src, seg, n):
    return jax.ops.segment_sum(src, seg, n)
kernel_name = 'mk_seq_postln_d1_jaxref_r8_d91f28'

def setup_inputs(seed: int=0):
    np.random.seed(seed)
    _w = jnp.asarray

    def _L0_attn_setup():
        import jax, jax.numpy as jnp
        import numpy as np
        HIDDEN = 256
        HEADS = 16
        HEAD_DIM = HIDDEN // HEADS
        NEG = -10000000000.0
        key = jax.random.key(seed)
        k1, k2, k3 = jax.random.split(key, 3)
        x = jax.random.normal(k1, (2, 256, HIDDEN), dtype=jnp.float32)
        w_qkv = jax.random.normal(k2, (HIDDEN, 3 * HIDDEN), dtype=jnp.float32) / np.sqrt(HIDDEN)
        w_out = jax.random.normal(k3, (HIDDEN, HIDDEN), dtype=jnp.float32) / np.sqrt(HIDDEN)
        return {'x': x, 'w_qkv': w_qkv, 'w_out': w_out}
    _L0_attn_in = _L0_attn_setup()

    def _L0_ffn_setup():
        import jax, jax.numpy as jnp
        import numpy as np
        E = 16
        D = 256
        H = 176
        HS = 2 * 176
        TOP_K = 6
        ROUTE_SCALE = 1.0
        key = jax.random.key(seed)
        ks = jax.random.split(key, 16)
        s = 0.02
        return {'x': jax.random.normal(ks[0], (4, 128, D), dtype=jnp.float32), 'gate_w': jax.random.normal(ks[1], (E, D), dtype=jnp.float32) * s, 'gate_b': jax.random.normal(ks[2], (E,), dtype=jnp.float32) * s, 'w1': jax.random.normal(ks[3], (E, H, D), dtype=jnp.float32) * s, 'b1': jax.random.normal(ks[4], (E, H), dtype=jnp.float32) * s, 'w2': jax.random.normal(ks[5], (E, D, H), dtype=jnp.float32) * s, 'b2': jax.random.normal(ks[6], (E, D), dtype=jnp.float32) * s, 'w3': jax.random.normal(ks[7], (E, H, D), dtype=jnp.float32) * s, 'b3': jax.random.normal(ks[8], (E, H), dtype=jnp.float32) * s, 'ws1': jax.random.normal(ks[9], (HS, D), dtype=jnp.float32) * s, 'bs1': jax.random.normal(ks[10], (HS,), dtype=jnp.float32) * s, 'ws2': jax.random.normal(ks[11], (D, HS), dtype=jnp.float32) * s, 'bs2': jax.random.normal(ks[12], (D,), dtype=jnp.float32) * s, 'ws3': jax.random.normal(ks[13], (HS, D), dtype=jnp.float32) * s, 'bs3': jax.random.normal(ks[14], (HS,), dtype=jnp.float32) * s}
    _L0_ffn_in = _L0_ffn_setup()
    _d = {'L0_attn_x': _L0_attn_in['x'], 'L0_attn_w_qkv': _L0_attn_in['w_qkv'], 'L0_attn_w_out': _L0_attn_in['w_out'], 'L0_ffn_gate_w': _L0_ffn_in['gate_w'], 'L0_ffn_gate_b': _L0_ffn_in['gate_b'], 'L0_ffn_w1': _L0_ffn_in['w1'], 'L0_ffn_b1': _L0_ffn_in['b1'], 'L0_ffn_w2': _L0_ffn_in['w2'], 'L0_ffn_b2': _L0_ffn_in['b2'], 'L0_ffn_w3': _L0_ffn_in['w3'], 'L0_ffn_b3': _L0_ffn_in['b3'], 'L0_ffn_ws1': _L0_ffn_in['ws1'], 'L0_ffn_bs1': _L0_ffn_in['bs1'], 'L0_ffn_ws2': _L0_ffn_in['ws2'], 'L0_ffn_bs2': _L0_ffn_in['bs2'], 'L0_ffn_ws3': _L0_ffn_in['ws3'], 'L0_ffn_bs3': _L0_ffn_in['bs3']}
    _x0 = _d['L0_attn_x']
    _d['L0_attn_x'] = jax.random.normal(jax.random.fold_in(jax.random.key(seed), 1), (8, 512, 256), dtype=_x0.dtype)
    del _x0
    return _d

def reference(L0_attn_x, L0_attn_w_qkv, L0_attn_w_out, L0_ffn_gate_w, L0_ffn_gate_b, L0_ffn_w1, L0_ffn_b1, L0_ffn_w2, L0_ffn_b2, L0_ffn_w3, L0_ffn_b3, L0_ffn_ws1, L0_ffn_bs1, L0_ffn_ws2, L0_ffn_bs2, L0_ffn_ws3, L0_ffn_bs3):

    def _L0_attn_ref(x, w_qkv, w_out):
        import jax, jax.numpy as jnp
        import numpy as np
        HIDDEN = 256
        HEADS = 16
        HEAD_DIM = HIDDEN // HEADS
        NEG = -10000000000.0
        b, s, _ = x.shape
        qkv = x @ w_qkv
        qkv = qkv.reshape(b, s, 3, HEADS, HEAD_DIM)
        q, k, v = (qkv[:, :, 0], qkv[:, :, 1], qkv[:, :, 2])
        scale = jnp.sqrt(jnp.float32(HEAD_DIM)).astype(x.dtype)
        q = q / scale
        scores = jnp.einsum('bqhd,bkhd->bhqk', q, k)
        causal_mask = jnp.arange(s)[:, None] >= jnp.arange(s)[None, :]
        scores = jnp.where(causal_mask[None, None], scores, NEG)
        attn = jax.nn.softmax(scores, axis=-1)
        out = jnp.einsum('bhqk,bkhd->bqhd', attn, v).reshape(b, s, HIDDEN)
        return out @ w_out

    def _L0_ffn_ref(x, gate_w, gate_b, w1, b1, w2, b2, w3, b3, ws1, bs1, ws2, bs2, ws3, bs3):
        import jax, jax.numpy as jnp
        import numpy as np
        E = 16
        D = 256
        H = 176
        HS = 2 * 176
        TOP_K = 6
        ROUTE_SCALE = 1.0
        shape = x.shape
        xf = x.reshape(-1, shape[-1])
        scores = xf @ gate_w.T
        probs = jax.nn.softmax(scores.astype(jnp.float32), axis=-1)
        biased = probs + gate_b
        _, idx = jax.lax.top_k(biased, TOP_K)
        weights = jnp.take_along_axis(probs, idx, axis=1) * ROUTE_SCALE
        weights = weights.astype(x.dtype)
        onehot = jax.nn.one_hot(idx, E, dtype=weights.dtype)
        cw = jnp.einsum('tk,tke->te', weights, onehot)

        def expert_step(y, params):
            W1, B1, W2, B2, W3, B3, c = params
            h = jax.nn.silu(xf @ W1.T + B1) * (xf @ W3.T + B3)
            out = h @ W2.T + B2
            return (y + c[:, None] * out, None)
        y0 = jnp.zeros_like(xf)
        y, _ = jax.lax.scan(expert_step, y0, (w1, b1, w2, b2, w3, b3, cw.T))
        z = jax.nn.silu(xf @ ws1.T + bs1) * (xf @ ws3.T + bs3) @ ws2.T + bs2
        return (y + z).reshape(shape)
    x = L0_attn_x
    x = _layernorm(x + _L0_attn_ref(x, L0_attn_w_qkv, L0_attn_w_out), axis=-1)
    x = _layernorm(x + _L0_ffn_ref(x, L0_ffn_gate_w, L0_ffn_gate_b, L0_ffn_w1, L0_ffn_b1, L0_ffn_w2, L0_ffn_b2, L0_ffn_w3, L0_ffn_b3, L0_ffn_ws1, L0_ffn_bs1, L0_ffn_ws2, L0_ffn_bs2, L0_ffn_ws3, L0_ffn_bs3), axis=-1)
    return x

_drawn_inputs = setup_inputs


def setup_inputs(seed=0):
    import zlib

    import numpy as np

    out = dict(_drawn_inputs(seed))
    spreads = {}
    factors = {'L0_ffn_gate_w': 8.0,
     'L0_ffn_gate_b': 8.0,
     'L0_ffn_w1': 8.0,
     'L0_ffn_b1': 8.0,
     'L0_ffn_w2': 8.0,
     'L0_ffn_b2': 26.424,
     'L0_ffn_w3': 8.0,
     'L0_ffn_b3': 8.0,
     'L0_ffn_ws1': 2.863,
     'L0_ffn_bs1': 23.304,
     'L0_ffn_ws2': 2.816,
     'L0_ffn_bs2': 14.499,
     'L0_ffn_ws3': 2.832,
     'L0_ffn_bs3': 25.831}
    for name, (base, spread) in spreads.items():
        noise = np.random.default_rng([zlib.crc32(name.encode()), seed]).standard_normal(out[name].shape)
        drawn = base * np.exp(spread * noise) if base else spread * noise
        out[name] = jnp.asarray(drawn.astype(out[name].dtype))
    for name, factor in factors.items():
        out[name] = (out[name] * factor).astype(out[name].dtype)
    return out
```

```python
from contextlib import ExitStack

import numpy as np

import concourse.bass as bass
from concourse import mybir

P = 128
B, S, D = 8, 512, 256
HEADS, HD = 16, 16
E, H, HS, TOP_K = 16, 176, 352, 6
KD = D // P
QT = S // P
GH = 4
NG = HEADS // GH
SUBS = 8
STACK = 6 * HD
SHIFT_ROWS = 3
Q_BLOCKS = (0, 0, 0, 1, 1, 2)
K_BLOCKS = (0, 1, 2, 0, 1, 0)
FILLS = 11
HT = -(-(E * H + HS) // P)
HT_ROUTED = E * H // P
EPS = 1e-5
MASKED = -1e30
TAKEN = -3.0e38
ABOVE_ALL = 3.3e38

SCORE_FILLS = (
    [(3, (h,)) for h in range(4)] + [(2, (h,)) for h in range(4)] + [(1, (0, 1)), (1, (2, 3)), (0, (0, 1, 2, 3))]
)
FILLS_OF_SUB = [(0, 1), (2,), (3, 4), (5,), (6, 7), (8,), (9,), (10,)]

MISC = {
    (0, 1): "q0", (0, 2): "m", (0, 3): "q1", (0, 4): "k0", (0, 5): "O", (0, 6): "k1", (0, 7): "t0",
    (1, 1): "t1", (1, 2): "m", (1, 4): "p0", (1, 5): "O", (1, 6): "p1", (1, 7): "v0",
    (2, 1): "v1", (2, 2): "m", (2, 3): "x0", (2, 4): "x1", (2, 5): "O", (2, 7): "r",
    (3, 2): "m", (3, 5): "O", (3, 6): "c",
}
NEXT_BATCH = ("q0", "q1", "k0", "k1", "v0", "v1")
BATCH_BEFORE = ("t0", "t1", "p0", "p1", "x0", "x1", "r", "c")
PROLOGUE = ["q0", "q1", "k0", "k1", "v0", "v1", "m"]
EPILOGUE = ["O", *BATCH_BEFORE]


def has(b, g, stage):
    first, last = isinstance(b, int) and b == 0, isinstance(b, int) and b == B - 1
    if first and (stage in BATCH_BEFORE or (stage == "O" and g == 0)):
        return False
    return not (last and (stage in NEXT_BATCH or (stage == "m" and g == NG - 1)))


MISC_FIRST = [k for k in MISC if has(0, k[0], MISC[k])]


def fill_no(b, key):
    if isinstance(b, int) and b == 0:
        return len(PROLOGUE) + MISC_FIRST.index(key) + 1
    keys = list(MISC)
    if isinstance(b, int) and b == B - 1:
        keys = [k for k in keys if has(b, k[0], MISC[k])]
    return (b - 1) * len(MISC) + (len(PROLOGUE) + len(MISC_FIRST) + keys.index(key) + 1)


FILLS_BEFORE_EPILOGUE = (
    len(PROLOGUE) + len(MISC_FIRST) + (B - 2) * len(MISC) + len([k for k in MISC if has(B - 1, k[0], MISC[k])])
)


def postln_layer(nc, xT, x, wqk, wv, wo, gw, gb, wt, b13, b2, out):
    fp32, f32r, bf16 = mybir.dt.float32, mybir.dt.float32r, mybir.dt.bfloat16
    ALU, ACT, AX = mybir.AluOpType, mybir.ActivationFunctionType, mybir.AxisListType

    ctx = ExitStack()
    phase_a = ExitStack()

    def sem(name):
        return ctx.enter_context(nc.semaphore(name))

    def sb(name, shape, dt=fp32, where=ctx):
        return where.enter_context(nc.sbuf_tensor(name, shape, dt))

    def sa(name, shape, dt=fp32):
        return sb(name, shape, dt, phase_a)

    with ctx:
        x1_d = nc.dram_tensor("x1_d", (B, P, QT, D), fp32).ap()
        x1T_d = nc.dram_tensor("x1T_d", (B, 2, P, KD, S), fp32).ap()
        c_d = nc.dram_tensor("c_d", (3, E, B, S), fp32).ap()

        ident = sb("ident", [P, P])
        half_neg = sb("half_neg", [P, QT])
        stats = sb("stats", [P, QT, 6])
        mean_var = sb("mean_var", [P, QT, 2])
        var_eps = sb("var_eps", [P, QT])
        rstd = sb("rstd", [P, QT])

        ident_bf = sa("ident_bf", [P, P], bf16)
        causal = sa("causal", [P, P], bf16)
        WQK = [sa(f"wqk_{n}", [P, KD, 4, P], f32r) for n in ("hi", "lo")]
        WV = [sa(f"wv_{n}", [P, KD, D], f32r) for n in ("hi", "lo")]
        WO = [sa(f"wo_{n}", [P, KD, D], f32r) for n in ("hi", "lo")]
        GW = sa("gw_hi_lo", [P, KD, 2 * E], f32r)
        gw_raw = sa("gw_raw", [P, KD, E])
        gate_b = sa("gate_b", [P, E])
        xT_raw = sa("xT_raw", [P, KD, S])
        XT = [sa(f"xT_{n}", [P, KD, S], f32r) for n in ("hi", "lo")]
        stack_q = [sa(f"stack_q{n}", [P, HEADS, S], bf16) for n in range(2)]
        stack_k = [sa(f"stack_k{n}", [P, HEADS, S], bf16) for n in range(2)]
        parts = [[sa(f"{n}_{p}", [P, 2, S], bf16) for p in ("h", "m", "l")] for n in ("q", "k")]
        rest = sa("rest", [P, 2, S])
        probs = [sa(f"probs{kt}", [P, GH, S - P * kt]) for kt in range(QT)]
        values = [sa(f"values{n}", [P, QT, HEADS, 32]) for n in range(2)]
        attn_T = sa("attn_T", [P, S])
        attn = sa("attn", [P, QT, D])
        recip = sa("recip", [P, QT, GH])
        rowmax = [sa(f"rowmax{n}", [P, GH, QT]) for n in range(2)]
        shift = sa("shift", [E, P])
        shift_rest = sa("shift_rest", [E, P])
        shift_parts = [[sa(f"shift_{p}{n}", [E, P], bf16) for p in ("h", "m", "l")] for n in range(2)]
        t_raw = sa("t_raw", [P, KD, S])
        t_hi = sa("t_hi", [P, KD, S], f32r)
        t_lo = sa("t_lo", [P, KD, S], f32r)
        x_res = sa("x_res", [P, QT, D])
        x1 = sa("x1", [P, QT, D])
        logit_lo = sa("logit_lo", [P, QT, E])
        logits = sa("logits", [P, QT, E])
        top = sa("top", [P, QT])
        expo = sa("expo", [P, QT, E])
        total = sa("total", [P, QT])
        gate = sa("gate", [P, QT, E])
        biased = sa("biased", [P, QT, E + 2])
        top8 = sa("top8", [P, QT, 8])
        marked = sa("marked", [P, QT, E + 2])
        weight = sa("weight", [P, QT, E])
        cT_raw = sa("cT_raw", [E, S])
        cT_hi = sa("cT_hi", [E, S], f32r)
        cT_lo = sa("cT_lo", [E, S], f32r)
        raw0 = probs[0][:].rearrange("p h t -> p (h t)")
        wqk_raw, wv_raw, wo_raw = raw0[:, 0:1024], raw0[:, 1024:1536], raw0[:, 1536:2048]
        phase_a.close()

        W = [sb(f"w_{n}", [P, HT, 6, P], f32r) for n in ("hi", "lo")]
        w_raw = [sb(f"w_raw{n}", [P, 6, P]) for n in range(2)]
        bias = sb("bias13", [P, 2, HT])
        B2 = [sb(f"b2_{n}", [2 * E + 1, D], f32r) for n in ("hi", "lo")]
        X1T = [sb(f"x1T_{n}", [P, 2, KD, S], f32r) for n in range(2)]
        CT = [sb(f"cT_{n}", [2 * E + 1, S], f32r) for n in range(2)]
        c_all = [sb(f"c_all{n}", [P, S]) for n in range(2)]
        gated = [sb(f"gated{n}", [P, S]) for n in range(2)]
        hidden = [sb(f"hidden{n}", [P, S]) for n in range(2)]
        b2_raw = hidden[1][0:2 * E + 1, 0:D]
        h_hi = [sb(f"h_hi{n}", [P, S], f32r) for n in range(2)]
        h_lo = [sb(f"h_lo{n}", [P, S], f32r) for n in range(2)]
        y_T = sb("y_T", [P, KD, S])
        x1_b = sb("x1_b", [P, QT, D])

        psum = ctx.enter_context(nc.psum_tensor("psum", [P, 8, S], fp32))
        st = [psum[:, 2 * n:2 * n + 2, :] for n in range(2)]
        sm = [psum[:, 4 + n, :] for n in range(2)]
        ov = psum[:, 6, :]
        misc = psum[:, 7, :]
        u_ps = [psum[:, n, :] for n in range(2)]
        v_ps = [psum[:, 2 + n, :] for n in range(2)]
        y_ps = [psum[:, 4 + n, :] for n in range(2)]
        tr_ps = [psum[:, 6 + n, :] for n in range(2)]

        w_loaded = sem("w_loaded")
        gw_loaded = sem("gw_loaded")
        xT_loaded = sem("xT_loaded")
        xres_loaded = sem("xres_loaded")
        cleared = sem("cleared")
        consts = sem("consts")
        w_hi_done = sem("w_hi_done")
        w_lo_done = sem("w_lo_done")
        xT_hi_done = sem("xT_hi_done")
        xT_lo_done = sem("xT_lo_done")
        misc_full = sem("misc_full")
        misc_free = sem("misc_free")
        part_h_done = sem("part_h_done")
        part_m_done = sem("part_m_done")
        part_l_done = sem("part_l_done")
        stack_loaded = sem("stack_loaded")
        sm_full = sem("sm_full")
        sm_free = sem("sm_free")
        shift_step = sem("shift_step")
        shift_loaded = sem("shift_loaded")
        st_full = sem("st_full")
        exp_done = sem("exp_done")
        mask_done = sem("mask_done")
        pv_done = sem("pv_done")
        attn_T_done = sem("attn_T_done")
        recip_done = sem("recip_done")
        t_lo_done = sem("t_lo_done")
        ln_step = sem("ln_step")
        rstd_step = sem("rstd_step")
        x1_done = sem("x1_done")
        x1_stored = sem("x1_stored")
        tail_free = sem("tail_free")
        router_step = sem("router_step")
        router_exp = sem("router_exp")
        cT_lo_done = sem("cT_lo_done")
        c_stored = sem("c_stored")
        passed_dve = sem("passed_dve")
        passed_pool = sem("passed_pool")
        passed_sp = sem("passed_sp")
        wt_loaded = [sem(f"wt_loaded{n}") for n in range(2)]
        small_loaded = sem("small_loaded")
        b2_step = sem("b2_step")
        wt_hi = sem("wt_hi")
        wt_lo = sem("wt_lo")
        x1T_loaded = [sem(f"x1T_loaded{n}") for n in range(2)]
        x1b_loaded = sem("x1b_loaded")
        c_all_loaded = [sem(f"c_all_loaded{n}") for n in range(2)]
        u_full = sem("u_full")
        v_full = sem("v_full")
        gated_done = sem("gated_done")
        v_used = sem("v_used")
        hidden_done = sem("hidden_done")
        h_hi_done = sem("h_hi_done")
        h_lo_done = sem("h_lo_done")
        down_done = sem("down_done")
        y_T_done = sem("y_T_done")
        tr_full = sem("tr_full")
        y_sum = sem("y_sum")
        ln2_step = sem("ln2_step")
        rstd2_step = sem("rstd2_step")
        y_done = sem("y_done")
        out_stored = sem("out_stored")

        block = ctx.enter_context(nc.Block())
        PARTS3 = ((0, 0), (0, 1), (1, 0))
        LAST = B - 1
        STEPS_R = 10

        def settle(eng, passed):
            eng.sem_inc(passed, 1)

        def by_two(eng, body, first, second_last):
            with eng.Fori(0, (second_last - first + 1) // 2) as turn:
                for k in range(2):
                    body(2 * turn + (first + k), (first + k) % 2)

        @block.sync
        def _(sp):
            sp.dma_start(xT_raw[:], xT[0]).then_inc(xT_loaded, 16)
            sp.dma_start(wqk_raw, wqk).then_inc(w_loaded, 16)
            sp.dma_start(wv_raw, wv).then_inc(w_loaded, 16)
            sp.dma_start(wo_raw, wo).then_inc(w_loaded, 16)
            sp.dma_start(gw_raw[:], gw).then_inc(gw_loaded, 16)
            sp.dma_start(gate_b[:], gb).then_inc(gw_loaded, 16)

            def load_stack(nb, par):
                for n, (dst, blocks) in enumerate(((stack_q[par], Q_BLOCKS), (stack_k[par], K_BLOCKS))):
                    sp.wait_ge(part_l_done, 4 * nb + (2 * n + 2))
                    for j, part in enumerate(blocks):
                        sp.dma_start(dst[HD * j:HD * j + HD, :, :], parts[n][part][:]).then_inc(stack_loaded, 16)

            def load_shift(G, par, gpar, g):
                sp.wait_ge(shift_step, 4 * G + 4)
                for j in range(SHIFT_ROWS):
                    sp.dma_start(
                        stack_q[par][STACK + j:STACK + j + 1, GH * g:GH * g + GH, :], shift_parts[gpar][j][:]
                    ).then_inc(shift_loaded, 16)

            def iteration(b, par):
                last = isinstance(b, int) and b == LAST
                first = isinstance(b, int) and b == 0
                if not last:
                    sp.wait_ge(xT_lo_done, b + 2)
                    sp.dma_start(xT_raw[:], xT[b + 2]).then_inc(xT_loaded, 16)
                load_shift(4 * b + 1, par, 1, 1)
                if not last:
                    if not first:
                        sp.wait_ge(st_full, 8 * 4 * b)
                    load_stack(b + 1, 1 - par)
                load_shift(4 * b + 2, par, 0, 2)
                if not first:
                    sp.wait_ge(x1_done, b)
                sp.dma_start(x_res[:], x[b]).then_inc(xres_loaded, 16)
                load_shift(4 * b + 3, par, 1, 3)
                if not first:
                    store_x1(b - 1)
                if not last:
                    load_shift(4 * b + 4, 1 - par, 0, 0)
                if not first:
                    store_c(b - 1)
                    sp.wait_ge(x1_stored, 48 * b)
                    sp.wait_ge(c_stored, 48 * b)
                    sp.sem_inc(tail_free, 1)

            def store_x1(t):
                sp.wait_ge(t_lo_done, 4 * t + 4)
                sp.dma_start(x1_d[t], x1[:]).then_inc(x1_stored, 16)
                sp.dma_start(x1T_d[t, 0], t_hi[:].bitcast(fp32)).then_inc(x1_stored, 16)
                sp.dma_start(x1T_d[t, 1], t_lo[:].bitcast(fp32)).then_inc(x1_stored, 16)

            def store_c(t):
                sp.wait_ge(cT_lo_done, t + 1)
                sp.dma_start(c_d[0, :, t, :], cT_raw[:]).then_inc(c_stored, 16)
                sp.dma_start(c_d[1, :, t, :], cT_hi[:].bitcast(fp32)).then_inc(c_stored, 16)
                sp.dma_start(c_d[2, :, t, :], cT_lo[:].bitcast(fp32)).then_inc(c_stored, 16)

            sp.sem_inc(tail_free, 1)
            load_stack(0, 0)
            sp.wait_ge(xT_lo_done, 1)
            sp.dma_start(xT_raw[:], xT[1]).then_inc(xT_loaded, 16)
            load_shift(0, 0, 0, 0)
            iteration(0, 0)
            by_two(sp, iteration, 1, LAST - 1)
            iteration(LAST, LAST % 2)
            store_x1(LAST)
            store_c(LAST)

            sp.wait_ge(x1_stored, 48 * B)
            sp.wait_ge(c_stored, 48 * B)
            sp.wait_ge(misc_full, FILLS_BEFORE_EPILOGUE + len(EPILOGUE))
            sp.wait_ge(misc_free, FILLS_BEFORE_EPILOGUE + len(EPILOGUE))

            def load_w(t):
                if t >= 2:
                    sp.wait_ge(wt_lo, t - 1)
                sp.dma_start(w_raw[t % 2][:], wt[t]).then_inc(wt_loaded[t % 2], 16)

            def load_chunk(c, par):
                sp.dma_start(X1T[par][:].bitcast(fp32), x1T_d[c].rearrange("n p k t -> p n k t")).then_inc(
                    x1T_loaded[par], 16)
                sp.dma_start(CT[par][0:E, :].bitcast(fp32), c_d[1, :, c, :]).then_inc(x1T_loaded[par], 16)
                sp.dma_start(CT[par][E:2 * E, :].bitcast(fp32), c_d[2, :, c, :]).then_inc(x1T_loaded[par], 16)

            def load_c_all(T, c, t, tpar):
                if not (isinstance(T, int) and T < 2):
                    sp.wait_ge(hidden_done, T - 1)
                    settle(sp, passed_sp)
                first_e, last_e = t * P // H, (t * P + P - 1) // H
                edge = last_e * H - t * P if last_e > first_e else P // 2
                for e, lo, hi in ((first_e, 0, edge), (last_e, edge, P)):
                    sp.dma_start(c_all[tpar][lo:hi, :], c_d[0, e, c, :].partition_broadcast(hi - lo)).then_inc(
                        c_all_loaded[tpar], 16)

            def chunk(c, par):
                whole = isinstance(c, int)
                for t in range(HT_ROUTED):
                    if whole and c == 0 and t + 2 < HT:
                        load_w(t + 2)
                    load_c_all(HT * c + t, c, t, (par + t) % 2)
                    if t == 4 and not (whole and c == LAST):
                        if not (whole and c == 0):
                            sp.wait_ge(y_T_done, 2 * c)
                        load_chunk(c + 1, 1 - par)
                    if t == 9:
                        if not (whole and c == 0):
                            sp.wait_ge(y_done, c)
                            store_out(c - 1)
                            sp.wait_ge(out_stored, 16 * c)
                        sp.dma_start(x1_b[:], x1_d[c]).then_inc(x1b_loaded, 16)
                for t in range(HT_ROUTED, HT - 2):
                    if whole and c == 0:
                        load_w(t + 2)

            def store_out(c):
                sp.dma_start(out[c], x1_b[:]).then_inc(out_stored, 16)

            load_w(0)
            load_w(1)
            load_chunk(0, 0)
            sp.dma_start(bias[:], b13).then_inc(small_loaded, 16)
            sp.dma_start(b2_raw, b2).then_inc(small_loaded, 16)
            chunk(0, 0)
            by_two(sp, chunk, 1, LAST - 1)
            chunk(LAST, LAST % 2)
            sp.wait_ge(y_done, B)
            store_out(LAST)
            sp.wait_ge(out_stored, 16 * B)

        @block.tensor
        def _(pe):
            def fill(n):
                if not (isinstance(n, int) and n == 1):
                    pe.wait_ge(misc_free, n - 1)

            def three_pass(dst, lhs, rhs):
                n = 0
                for k in range(KD):
                    for a, b in PARTS3:
                        last = nc.tensor.matmul(dst, lhs(a, k), rhs(b, k), start=n == 0, stop=n == 3 * KD - 1)
                        n += 1
                return last

            def scores_for_max(G, par, g, f):
                n = FILLS * G + f
                bank = (g + f) % 2
                if not (isinstance(n, int) and n < 2):
                    pe.wait_ge(sm_free, n - 1)
                qt, heads = SCORE_FILLS[f]
                width = P * (qt + 1)
                for i, h in enumerate(heads):
                    head = GH * g + h
                    dst = sm[bank][:, i * width:(i + 1) * width]
                    nc.tensor.matmul(dst, stack_q[par][0:STACK, head, qt * P:qt * P + P],
                                     stack_k[par][0:STACK, head, 0:width], start=True, stop=False)
                    last = nc.tensor.matmul(dst[:, width - P:width], ident_bf[:], causal[:], start=False, stop=True)
                last.then_inc(sm_full, 1)

            def scores(G, par, g, s):
                kt, pair = s // 2, s % 2
                n = 8 * G + s
                if not (isinstance(n, int) and n < 2):
                    pe.wait_ge(exp_done, n - 1)
                for i in range(2):
                    head = GH * g + 2 * pair + i
                    last = nc.tensor.matmul(st[s % 2][:, i, 0:S - kt * P],
                                            stack_k[par][0:STACK + SHIFT_ROWS, head, kt * P:kt * P + P],
                                            stack_q[par][0:STACK + SHIFT_ROWS, head, kt * P:S],
                                            start=True, stop=True)
                last.then_inc(st_full, 1)

            def attend(G, par, g, kt):
                if kt == 0 and not (isinstance(G, int) and G == 0):
                    pe.wait_ge(attn_T_done, G)
                pe.wait_ge(mask_done, 4 * G + (kt + 1))
                for j in range(GH):
                    last = nc.tensor.matmul(ov[32 * j:32 * j + 32, kt * P:S], values[par][:, kt, GH * g + j, :],
                                            probs[kt][:, j, :], start=kt == 0, stop=kt == QT - 1,
                                            skip_group_check=True)
                last.then_inc(pv_done, 1)

            def project_qk(nb, tile):
                if tile == 0:
                    pe.wait_ge(xT_lo_done, nb + 1)
                three_pass(misc, lambda a, k: WQK[a][:, k, tile, :], lambda b, k: XT[b][:, k, :]).then_inc(
                    misc_full, 1)

            def project_v(f):
                for j in range(2):
                    qt = 2 * f + j
                    last = three_pass(misc[:, j * D:j * D + D], lambda a, k: XT[a][:, k, qt * P:qt * P + P],
                                      lambda b, k: WV[b][:, k, :])
                last.then_inc(misc_full, 1)

            def transpose_max(G, gpar):
                pe.wait_ge(sm_free, FILLS * G + FILLS)
                nc.tensor.transpose(misc[0:E, 0:P], rowmax[gpar][:].rearrange("p h q -> p (h q)"), ident[:]).then_inc(
                    misc_full, 1)

            def transpose_out(G):
                pe.wait_ge(attn_T_done, G + 1)
                for qt in range(QT):
                    last = nc.tensor.transpose(misc[:, qt * P:qt * P + P], attn_T[:, qt * P:qt * P + P], ident[:])
                last.then_inc(misc_full, 1)

            def transpose_rows(src, k):
                for qt in range(QT):
                    last = nc.tensor.transpose(misc[:, qt * P:qt * P + P], src[:, qt, k * P:k * P + P], ident[:])
                last.then_inc(misc_full, 1)

            def project_out(t, f):
                pe.wait_ge(t_lo_done, 4 * t + 2)
                for j in range(2):
                    qt = 2 * f + j
                    last = three_pass(misc[:, j * D:j * D + D],
                                      lambda a, k: (t_hi, t_lo)[a][:, k, qt * P:qt * P + P],
                                      lambda b, k: WO[b][:, k, :])
                last.then_inc(misc_full, 1)

            def route(t):
                pe.wait_ge(t_lo_done, 4 * t + 4)
                for qt in range(QT):
                    dst = misc[:, 2 * E * qt:2 * E * qt + 2 * E]
                    for k in range(KD):
                        nc.tensor.matmul(dst, t_hi[:, k, qt * P:qt * P + P], GW[:, k, :], start=k == 0, stop=False)
                    for k in range(KD):
                        last = nc.tensor.matmul(dst[:, 0:E], t_lo[:, k, qt * P:qt * P + P], GW[:, k, 0:E],
                                                start=False, stop=k == KD - 1)
                last.then_inc(misc_full, 1)

            def transpose_weights(t):
                pe.wait_ge(router_step, STEPS_R * (t + 1))
                for qt in range(QT):
                    last = nc.tensor.transpose(misc[0:E, qt * P:qt * P + P], weight[:, qt, :], ident[:])
                last.then_inc(misc_full, 1)

            def misc_stage(b, g, stage):
                if stage[0] in "qk":
                    project_qk(b + 1, ("q0", "q1", "k0", "k1").index(stage))
                elif stage[0] == "v":
                    project_v(int(stage[1]))
                elif stage == "m":
                    transpose_max(4 * b + (g + 1), (g + 1) % 2)
                elif stage == "O":
                    transpose_out(4 * b + (g - 1))
                elif stage[0] == "t":
                    transpose_rows(attn, int(stage[1]))
                elif stage[0] == "p":
                    project_out(b - 1, int(stage[1]))
                elif stage[0] == "x":
                    if stage == "x0":
                        pe.wait_ge(x1_done, b)
                    transpose_rows(x1, int(stage[1]))
                elif stage == "r":
                    route(b - 1)
                else:
                    transpose_weights(b - 1)

            def iteration(b, par):
                whole = isinstance(b, int)
                for g in range(NG):
                    G = 4 * b + g
                    pe.wait_ge(stack_loaded, 192 * (b + 1))
                    pe.wait_ge(shift_loaded, 48 * (G + 1))
                    for s in range(SUBS):
                        scores(G, par, g, s)
                        if not (whole and 4 * b + g + 2 >= NG * B):
                            if g == 2 and s == 0:
                                pe.wait_ge(stack_loaded, 192 * (b + 2))
                            for f in FILLS_OF_SUB[s]:
                                scores_for_max(G + 2, par if g < 2 else 1 - par, (g + 2) % NG, f)
                        if s in (0, 2) and not (whole and b == 0 and g == 0):
                            attend(G - 1, par if g else 1 - par, (g - 1) % NG, 2 + s // 2)
                        if s in (4, 6):
                            attend(G, par, g, s // 2 - 2)
                        stage = MISC.get((g, s))
                        if stage and has(b, g, stage):
                            fill(fill_no(b, (g, s)))
                            misc_stage(b, g, stage)

            pe.wait_ge(consts, 5)
            pe.wait_ge(w_hi_done, 4)
            pe.wait_ge(w_lo_done, 4)
            for n, stage in enumerate(PROLOGUE[:-1]):
                fill(n + 1)
                misc_stage(-1, 3, stage)
            pe.wait_ge(stack_loaded, 192)
            for G in range(2):
                for f in range(FILLS):
                    scores_for_max(G, 0, G, f)
            fill(len(PROLOGUE))
            transpose_max(0, 0)
            iteration(0, 0)
            by_two(pe, iteration, 1, LAST - 1)
            iteration(LAST, LAST % 2)
            for kt in (2, 3):
                attend(NG * B - 1, LAST % 2, NG - 1, kt)
            for n, stage in enumerate(EPILOGUE):
                fill(FILLS_BEFORE_EPILOGUE + n + 1)
                misc_stage(B, 0, stage)

            def up(T, t, par, tpar):
                for ps, full, used, first in ((u_ps, u_full, gated_done, 0), (v_ps, v_full, v_used, 2)):
                    if not (isinstance(T, int) and T < 2):
                        pe.wait_ge(used, T - 1)
                    three_pass(ps[tpar], lambda a, k: W[a][:, t, first + k, :],
                               lambda b, k: X1T[par][:, b, k, :]).then_inc(full, 1)

            def down(T, t, tpar):
                pe.wait_ge(h_lo_done, T + 1)
                for d in range(KD):
                    for n, (a, b) in enumerate(PARTS3):
                        last = nc.tensor.matmul(y_ps[d], W[a][:, t, 4 + d, :], (h_hi, h_lo)[b][tpar][:],
                                                start=t == 0 and n == 0, stop=False, skip_group_check=True)
                last.then_inc(down_done, 1)

            def down_bias(par):
                for d in range(KD):
                    for a in range(2):
                        last = nc.tensor.matmul(y_ps[d], B2[a][:, d * P:d * P + P], CT[par][:], start=False,
                                                stop=a == 1, skip_group_check=True)
                last.then_inc(down_done, 1)

            def y_rows(c, f):
                if f == 0:
                    pe.wait_ge(y_T_done, 2 * c + 2)
                for j in range(2):
                    for d in range(KD):
                        qt = 2 * f + j
                        last = nc.tensor.transpose(tr_ps[f][:, j * D + d * P:j * D + d * P + P],
                                                   y_T[:, d, qt * P:qt * P + P], ident[:])
                last.then_inc(tr_full, 1)

            def chunk(c, par):
                whole = isinstance(c, int)
                first = whole and c == 0
                for t in range(HT):
                    T = HT * c + t
                    if first:
                        pe.wait_ge(wt_hi, t + 1)
                        pe.wait_ge(wt_lo, t + 1)
                    if t == 0:
                        pe.wait_ge(x1T_loaded[par], (c + (2 - par)) * 24)
                    up(T, t, par, (par + t) % 2)
                    if t >= 2:
                        if t == 2 and not first:
                            pe.wait_ge(y_T_done, 2 * c)
                        down(T - 2, t - 2, (par + t) % 2)
                    elif not first:
                        down(T - 2, HT - 2 + t, (par + t) % 2)
                        if t == 1:
                            down_bias(1 - par)
                    if not first and t in (4, 5):
                        y_rows(c - 1, t - 4)

            pe.wait_ge(b2_step, 3)
            chunk(0, 0)
            by_two(pe, chunk, 1, LAST - 1)
            chunk(LAST, LAST % 2)
            for t in (HT - 2, HT - 1):
                T = HT * LAST + t
                down(T, t, T % 2)
            down_bias(LAST % 2)
            for f in range(2):
                y_rows(LAST, f)

        @block.scalar
        def _(act):
            def copy(dst, src, scale=1.0):
                return nc.scalar.activation(dst, src, ACT.Copy, scale=scale)

            def probabilities(G, s):
                kt, pair = s // 2, s % 2
                act.wait_ge(st_full, 8 * G + (s + 1))
                if not (isinstance(G, int) and G == 0):
                    act.wait_ge(pv_done, 4 * G + (kt - 3))
                nc.scalar.activation(probs[kt][:, 2 * pair:2 * pair + 2, :], st[s % 2][:, :, 0:S - kt * P],
                                     ACT.Exp).then_inc(exp_done, 1)

            def split_x(nb):
                act.wait_ge(xT_loaded, 16 * (nb + 1))
                copy(XT[0][:], xT_raw[:]).then_inc(xT_hi_done, 1)

            def transposed(k):
                copy(t_hi[:, k, :], misc)
                copy(t_raw[:, k, :], misc).then_inc(misc_free, 1)

            def misc_stage(b, g, stage, n):
                t = b - 1
                if stage in ("p0", "p1", "r", "O"):
                    return
                act.wait_ge(misc_full, n)
                if stage[0] in "qk":
                    tile = ("q0", "q1", "k0", "k1").index(stage)
                    if tile == 0 and not (isinstance(b, int) and b == -1):
                        act.wait_ge(stack_loaded, 192 * (b + 1))
                    copy(parts[tile // 2][0][:, tile % 2, :], misc, 0.25 if tile < 2 else 1.0).then_inc(
                        part_h_done, 1)
                elif stage[0] == "v":
                    f = int(stage[1])
                    dst = values[(b + 1) % 2 if isinstance(b, int) else g][:, 2 * f:2 * f + 2, :, 0:HD]
                    copy(dst, misc.rearrange("p (q h d) -> p q h d", q=2, h=HEADS)).then_inc(misc_free, 1)
                elif stage == "m":
                    G = 4 * b + (g + 1)
                    if not (isinstance(G, int) and G == 0):
                        act.wait_ge(shift_step, 4 * G)
                    copy(shift[:], misc[0:E, 0:P], -1.0).then_inc(misc_free, 1)
                elif stage[0] == "t":
                    k = int(stage[1])
                    if k == 0:
                        act.wait_ge(tail_free, t + 1)
                    transposed(k)
                elif stage[0] == "x":
                    k = int(stage[1])
                    act.wait_ge(t_lo_done, 4 * t + (k + 1))
                    transposed(k)
                elif stage == "c":
                    copy(cT_hi[:], misc[0:E, :])
                    copy(cT_raw[:], misc[0:E, :]).then_inc(misc_free, 1)

            def read_attn(G):
                act.wait_ge(pv_done, 4 * G + 4)
                if not (isinstance(G, int) and G == 0):
                    act.wait_ge(recip_done, G)
                copy(attn_T[:], ov).then_inc(attn_T_done, 1)

            def router_softmax(t):
                act.wait_ge(router_step, STEPS_R * t + 3)
                nc.scalar.activation(expo[:], logits[:], ACT.Exp).then_inc(router_exp, 1)

            def iteration(b, par):
                whole = isinstance(b, int)
                for g in range(NG):
                    G = 4 * b + g
                    for s in range(SUBS):
                        probabilities(G, s)
                        if s == 3 and not (whole and b == 0 and g == 0):
                            read_attn(G - 1)
                        stage = MISC.get((g, s))
                        if stage and has(b, g, stage):
                            misc_stage(b, 1 - par if stage[0] == "v" else g, stage, fill_no(b, (g, s)))
                        if (g, s) == (3, 1) and not (whole and b == 0):
                            router_softmax(b - 1)
                        if (g, s) == (3, 4) and not (whole and b == LAST):
                            split_x(b + 2)

            split_x(0)
            act.wait_ge(w_loaded, 48)
            copy(WQK[0][:].rearrange("p k t m -> p (k t m)"), wqk_raw).then_inc(w_hi_done, 1)
            copy(WV[0][:].rearrange("p k n -> p (k n)"), wv_raw).then_inc(w_hi_done, 1)
            copy(WO[0][:].rearrange("p k n -> p (k n)"), wo_raw).then_inc(w_hi_done, 1)
            act.wait_ge(gw_loaded, 32)
            copy(GW[:, :, 0:E], gw_raw[:]).then_inc(w_hi_done, 1)
            for n, stage in enumerate(PROLOGUE[:-1]):
                misc_stage(-1, 0, stage, n + 1)
            act.wait_ge(misc_full, len(PROLOGUE) - 1)
            split_x(1)
            misc_stage(-1, 3, "m", len(PROLOGUE))
            act.wait_ge(w_lo_done, 4)
            iteration(0, 0)
            by_two(act, iteration, 1, LAST - 1)
            iteration(LAST, LAST % 2)
            read_attn(NG * B - 1)
            for n, stage in enumerate(EPILOGUE):
                if stage == "c":
                    router_softmax(LAST)
                misc_stage(B, 0, stage, FILLS_BEFORE_EPILOGUE + n + 1)

            def split_w(t):
                act.wait_ge(wt_loaded[t % 2], 16 * (t // 2 + 1))
                copy(W[0][:, t], w_raw[t % 2][:]).then_inc(wt_hi, 1)

            def silu(T, t, tpar):
                act.wait_ge(u_full, T + 1)
                if not (isinstance(T, int) and T < 2):
                    act.wait_ge(v_used, T - 1)
                nc.scalar.activation(gated[tpar][:], u_ps[tpar], ACT.Silu, bias=bias[:, 0, t:t + 1]).then_inc(
                    gated_done, 1)

            def read_y(c):
                act.wait_ge(down_done, (HT + 1) * (c + 1))
                for d in range(KD):
                    copy(y_T[:, d, :], y_ps[d]).then_inc(y_T_done, 1)

            def high(c, t, tpar):
                T = HT * c + t
                act.wait_ge(hidden_done, T + 1)
                if not (isinstance(T, int) and T < 2):
                    act.wait_ge(down_done, (HT + 1) * c + (t - 1 if t >= 2 else t - 2))
                copy(h_hi[tpar][:], hidden[tpar][:]).then_inc(h_hi_done, 1)

            def chunk(c, par):
                first = isinstance(c, int) and c == 0
                for t in range(HT):
                    if first and t + 2 < HT:
                        split_w(t + 2)
                    silu(HT * c + t, t, (par + t) % 2)
                    if not (first and t == 0):
                        high(c, t - 1, (par + t + 1) % 2)
                    if t == 2 and not first:
                        read_y(c - 1)

            act.wait_ge(small_loaded, 32)
            copy(B2[0][:], b2_raw).then_inc(b2_step, 1)
            split_w(0)
            split_w(1)
            chunk(0, 0)
            by_two(act, chunk, 1, LAST - 1)
            chunk(LAST, LAST % 2)
            high(LAST, HT - 1, (LAST + HT - 1) % 2)
            read_y(LAST)

        @block.vector
        def _(dve):
            def maxima(G, g, f, gpar):
                qt, heads = SCORE_FILLS[f]
                width, n = P * (qt + 1), len(heads)
                dve.wait_ge(sm_full, FILLS * G + (f + 1))
                src = sm[(g + f) % 2][:, 0:n * width].rearrange("p (h k) -> p h k", h=n)
                nc.vector.reduce_max(rowmax[gpar][:, heads[0]:heads[0] + n, qt], src, AX.X).then_inc(
                    sm_free, 1)

            def layer_norm_stats(src, f, step, base):
                for qt in (2 * f, 2 * f + 1):
                    last = nc.vector.bn_stats(stats[:, qt, :], src[:, qt, :])
                last.then_inc(step, 1)
                dve.wait_ge(step, base + (2 * f + 1))
                settle(dve, passed_dve)
                for qt in (2 * f, 2 * f + 1):
                    last = nc.vector.bn_aggr(mean_var[:, qt, :], stats[:, qt, :])
                last.then_inc(step, 1)

            def normalize(buf, done):
                for qt in range(QT):
                    last = nc.vector.tensor_scalar(buf[:, qt, :], buf[:, qt, :], mean_var[:, qt, 0:1],
                                                   rstd[:, qt:qt + 1], ALU.subtract, ALU.mult)
                last.then_inc(done, 1)

            def misc_stage(b, g, stage, n):
                t = b - 1
                if stage[0] in "qk":
                    tile = ("q0", "q1", "k0", "k1").index(stage)
                    m = 4 * (b + 1) + tile
                    dve.wait_ge(part_h_done, m + 1)
                    if not (isinstance(m, int) and m < 2):
                        dve.wait_ge(part_l_done, m - 1)
                    nc.vector.scalar_tensor_tensor(rest[:, tile % 2, :], misc, 0.25 if tile < 2 else 1.0,
                                                   parts[tile // 2][0][:, tile % 2, :], ALU.mult,
                                                   ALU.subtract).then_inc(misc_free, 1)
                elif stage == "O":
                    G = 4 * b + (g - 1)
                    dve.wait_ge(misc_full, n)
                    rows = misc.rearrange("p (q h c) -> p q h c", q=QT, h=GH)
                    nc.vector.reciprocal(recip[:], rows[:, :, :, HD]).then_inc(recip_done, 1)
                    dve.wait_ge(recip_done, G + 1)
                    dst = attn[:, :, ((g - 1) % NG) * GH * HD:((g - 1) % NG + 1) * GH * HD]
                    nc.vector.tensor_tensor(dst.rearrange("p q (h d) -> p q h d", h=GH), rows[:, :, :, 0:HD],
                                            recip[:].unsqueeze(3).to_broadcast([P, QT, GH, HD]),
                                            ALU.mult).then_inc(misc_free, 1)
                elif stage[0] == "p":
                    f = int(stage[1])
                    dve.wait_ge(misc_full, n)
                    if f == 0:
                        dve.wait_ge(xres_loaded, 16 * (t + 1))
                    nc.vector.tensor_tensor(x1[:, 2 * f:2 * f + 2, :],
                                            misc.rearrange("p (q d) -> p q d", q=2),
                                            x_res[:, 2 * f:2 * f + 2, :], ALU.add).then_inc(misc_free, 1)
                    dve.wait_ge(misc_free, n)
                    layer_norm_stats(x1, f, ln_step, 4 * t)
                elif stage == "r":
                    dve.wait_ge(misc_full, n)
                    route(t)

            def route(t):
                step = [STEPS_R * t]

                def then(ins):
                    step[0] = step[0] + 1
                    ins.then_inc(router_step, 1)
                    dve.wait_ge(router_step, step[0])

                rows = misc[:, 0:2 * E * QT].rearrange("p (q e) -> p q e", q=QT)
                then(nc.vector.tensor_copy(logit_lo[:], rows[:, :, E:2 * E]))
                nc.vector.tensor_tensor(logits[:], rows[:, :, 0:E], logit_lo[:], ALU.add).then_inc(misc_free, 1)

            def route_max(t, n):
                dve.wait_ge(misc_free, n)
                nc.vector.reduce_max(top[:], logits[:], AX.X).then_inc(router_step, 1)
                dve.wait_ge(router_step, STEPS_R * t + 2)
                nc.vector.tensor_tensor(logits[:], logits[:], top[:].unsqueeze(2).to_broadcast([P, QT, E]),
                                        ALU.subtract).then_inc(router_step, 1)

            def route_top(t):
                step = [STEPS_R * t + 3]

                def then(ins):
                    step[0] = step[0] + 1
                    ins.then_inc(router_step, 1)
                    dve.wait_ge(router_step, step[0])

                dve.wait_ge(router_exp, t + 1)
                then(nc.vector.reduce_sum(total[:], expo[:], AX.X))
                then(nc.vector.reciprocal(total[:], total[:]))
                then(nc.vector.tensor_tensor(gate[:], expo[:], total[:].unsqueeze(2).to_broadcast([P, QT, E]),
                                             ALU.mult))
                then(nc.vector.tensor_tensor(biased[:, :, 0:E], gate[:],
                                             gate_b[:].unsqueeze(1).to_broadcast([P, QT, E]), ALU.add))
                settle(dve, passed_dve)
                for qt in range(QT):
                    last = nc.vector.max(top8[:, qt, :], biased[:, qt, :])
                then(last)
                settle(dve, passed_dve)
                for qt in range(QT):
                    last = nc.vector.match_replace(marked[:, qt, :], top8[:, qt, :], biased[:, qt, :], TAKEN)
                then(last)
                nc.vector.scalar_tensor_tensor(weight[:], marked[:, :, 0:E], TAKEN, gate[:], ALU.is_equal,
                                               ALU.mult).then_inc(router_step, 1)

            def iteration(b, par):
                whole = isinstance(b, int)
                for g in range(NG):
                    G = 4 * b + g
                    for s in range(SUBS):
                        if not (whole and 4 * b + g + 2 >= NG * B):
                            for f in FILLS_OF_SUB[s]:
                                maxima(G + 2, (g + 2) % NG, f, g % 2)
                        stage = MISC.get((g, s))
                        if stage and has(b, g, stage):
                            misc_stage(b, g, stage, fill_no(b, (g, s)))
                        if not (whole and b == 0):
                            if (g, s) == (2, 0):
                                dve.wait_ge(rstd_step, 2 * b)
                                normalize(x1, x1_done)
                            if (g, s) == (2, 7):
                                route_max(b - 1, fill_no(b, (2, 7)))
                            if (g, s) == (3, 2):
                                route_top(b - 1)

            nc.vector.memset(biased[:, :, E:E + 2], ABOVE_ALL).then_inc(cleared, 1)
            for n in range(2):
                nc.vector.memset(stack_k[n][STACK:STACK + SHIFT_ROWS, :, :], 1.0).then_inc(cleared, 1)
            dve.wait_ge(w_hi_done, 3)
            for (hi, lo), raw, names in ((WQK, wqk_raw, "p k t m -> p (k t m)"), (WV, wv_raw, "p k n -> p (k n)"),
                                         (WO, wo_raw, "p k n -> p (k n)")):
                nc.vector.tensor_tensor(lo[:].rearrange(names), raw, hi[:].bitcast(fp32).rearrange(names),
                                        ALU.subtract).then_inc(w_lo_done, 1)
            dve.wait_ge(w_hi_done, 4)
            nc.vector.tensor_tensor(GW[:, :, E:2 * E], gw_raw[:], GW[:, :, 0:E].bitcast(fp32),
                                    ALU.subtract).then_inc(w_lo_done, 1)
            for n, stage in enumerate(PROLOGUE[:-1]):
                if stage[0] in "qk":
                    misc_stage(-1, 0, stage, n + 1)
            for G in range(2):
                for f in range(FILLS):
                    maxima(G, G, f, G)
            iteration(0, 0)
            by_two(dve, iteration, 1, LAST - 1)
            iteration(LAST, LAST % 2)
            for n, stage in enumerate(EPILOGUE):
                no = FILLS_BEFORE_EPILOGUE + n + 1
                misc_stage(B, 0, stage, no)
                if stage == "p1":
                    dve.wait_ge(rstd_step, 2 * B)
                    normalize(x1, x1_done)
                if stage == "r":
                    route_max(LAST, no)
                    route_top(LAST)

            def split_w(t):
                dve.wait_ge(wt_hi, t + 1)
                nc.vector.tensor_tensor(W[1][:, t], w_raw[t % 2][:], W[0][:, t].bitcast(fp32),
                                        ALU.subtract).then_inc(wt_lo, 1)

            def hide(c, T, t, tpar):
                dve.wait_ge(gated_done, T + 1)
                dve.wait_ge(v_full, T + 1)
                if not (isinstance(T, int) and T < 2):
                    dve.wait_ge(h_lo_done, T - 1)
                routed = t < HT_ROUTED
                nc.vector.scalar_tensor_tensor(hidden[tpar][:], v_ps[tpar], bias[:, 1, t:t + 1], gated[tpar][:],
                                               ALU.add, ALU.mult).then_inc(v_used, 1)
                dve.wait_ge(v_used, T + 1)
                if routed:
                    par0 = (tpar - t) % 2
                    own = [n for n in range(HT_ROUTED) if (par0 + n) % 2 == tpar]
                    half = HT_ROUTED // 2
                    dve.wait_ge(c_all_loaded[tpar], 32 * (c * half) + 32 * (own.index(t) + 1))
                    nc.vector.tensor_tensor(hidden[tpar][:], hidden[tpar][:], c_all[tpar][:],
                                            ALU.mult).then_inc(hidden_done, 1)
                else:
                    settle(dve, passed_dve)
                    dve.engine_nop().then_inc(hidden_done, 1)

            def add_x1(c, f):
                dve.wait_ge(tr_full, 2 * c + (f + 1))
                dve.wait_ge(x1b_loaded, 16 * (c + 1))
                nc.vector.tensor_tensor(x1_b[:, 2 * f:2 * f + 2, :], tr_ps[f].rearrange("p (q d) -> p q d", q=2),
                                        x1_b[:, 2 * f:2 * f + 2, :], ALU.add).then_inc(y_sum, 1)
                dve.wait_ge(y_sum, 2 * c + (f + 1))
                layer_norm_stats(x1_b, f, ln2_step, 4 * c)

            def finish(c):
                dve.wait_ge(rstd2_step, 2 * c + 2)
                normalize(x1_b, y_done)

            def chunk(c, par):
                first = isinstance(c, int) and c == 0
                for t in range(HT):
                    if first and t + 2 < HT:
                        split_w(t + 2)
                    hide(c, HT * c + t, t, (par + t) % 2)
                    if not first and t in (4, 5):
                        add_x1(c - 1, t - 4)
                    if not first and t == 7:
                        finish(c - 1)

            dve.wait_ge(b2_step, 1)
            nc.vector.tensor_tensor(B2[1][:], b2_raw, B2[0][:].bitcast(fp32), ALU.subtract).then_inc(b2_step, 1)
            split_w(0)
            split_w(1)
            for n in range(2):
                last = nc.vector.memset(CT[n][2 * E:2 * E + 1, :].bitcast(fp32), 1.0)
            last.then_inc(b2_step, 1)
            chunk(0, 0)
            by_two(dve, chunk, 1, LAST - 1)
            chunk(LAST, LAST % 2)
            for f in range(2):
                add_x1(LAST, f)
            finish(LAST)

        @block.gpsimd
        def _(pool):
            def mask(G, kt):
                pool.wait_ge(exp_done, 8 * G + (2 * kt + 2))
                settle(pool, passed_pool)
                diag = probs[kt][:, :, 0:P]
                nc.gpsimd.affine_select(out=diag, in_=diag, pattern=[[0, GH], [1, P]], compare_op=ALU.is_ge,
                                        fill=0.0, base=0, channel_multiplier=-1).then_inc(mask_done, 1)

            def split_x(nb):
                pool.wait_ge(xT_hi_done, nb + 1)
                nc.gpsimd.tensor_tensor(XT[1][:], xT_raw[:], XT[0][:].bitcast(fp32), ALU.subtract).then_inc(
                    xT_lo_done, 1)

            def misc_stage(b, g, stage, n):
                t = b - 1
                if stage[0] in "qk":
                    tile = ("q0", "q1", "k0", "k1").index(stage)
                    m = 4 * (b + 1) + tile
                    part, half = parts[tile // 2], tile % 2
                    pool.wait_ge(misc_free, n)
                    settle(pool, passed_pool)
                    nc.gpsimd.tensor_copy(part[1][:, half, :], rest[:, half, :]).then_inc(part_m_done, 1)
                    pool.wait_ge(part_m_done, m + 1)
                    nc.gpsimd.tensor_tensor(part[2][:, half, :], rest[:, half, :], part[1][:, half, :],
                                            ALU.subtract).then_inc(part_l_done, 1)
                elif stage == "m":
                    G = 4 * b + (g + 1)
                    high, mid, low = shift_parts[(g + 1) % 2]
                    pool.wait_ge(misc_free, n)
                    if not (isinstance(G, int) and G < 2):
                        pool.wait_ge(shift_loaded, 48 * (G - 1))
                    settle(pool, passed_pool)
                    nc.gpsimd.tensor_copy(high[:], shift[:]).then_inc(shift_step, 1)
                    pool.wait_ge(shift_step, 4 * G + 1)
                    nc.gpsimd.tensor_tensor(shift_rest[:], shift[:], high[:], ALU.subtract).then_inc(shift_step, 1)
                    pool.wait_ge(shift_step, 4 * G + 2)
                    settle(pool, passed_pool)
                    nc.gpsimd.tensor_copy(mid[:], shift_rest[:]).then_inc(shift_step, 1)
                    pool.wait_ge(shift_step, 4 * G + 3)
                    nc.gpsimd.tensor_tensor(low[:], shift_rest[:], mid[:], ALU.subtract).then_inc(shift_step, 1)
                elif stage[0] in "tx":
                    k = int(stage[1])
                    pool.wait_ge(misc_free, n)
                    nc.gpsimd.tensor_tensor(t_lo[:, k, :], t_raw[:, k, :], t_hi[:, k, :].bitcast(fp32),
                                            ALU.subtract).then_inc(t_lo_done, 1)
                elif stage == "c":
                    pool.wait_ge(misc_free, n)
                    nc.gpsimd.tensor_tensor(cT_lo[:], cT_raw[:], cT_hi[:].bitcast(fp32), ALU.subtract).then_inc(
                        cT_lo_done, 1)

            def inverse_std(ready, step, c):
                pool.wait_ge(ready, 4 * c + 4)
                settle(pool, passed_pool)
                nc.gpsimd.tensor_scalar(var_eps[:], mean_var[:, :, 1], EPS, None, ALU.add).then_inc(step, 1)
                pool.wait_ge(step, 2 * c + 1)
                nc.gpsimd.tensor_tensor(rstd[:], var_eps[:], half_neg[:], ALU.pow).then_inc(step, 1)

            def iteration(b, par):
                whole = isinstance(b, int)
                for g in range(NG):
                    G = 4 * b + g
                    for s in range(SUBS):
                        if s % 2:
                            mask(G, s // 2)
                        stage = MISC.get((g, s))
                        if stage and has(b, g, stage):
                            misc_stage(b, g, stage, fill_no(b, (g, s)))
                        if (g, s) == (1, 7) and not (whole and b == 0):
                            inverse_std(ln_step, rstd_step, b - 1)
                        if (g, s) == (3, 4) and not (whole and b == LAST):
                            split_x(b + 2)

            nc.gpsimd.memset(ident[:], 0.0).then_inc(cleared, 1)
            nc.gpsimd.memset(ident_bf[:], 0.0).then_inc(cleared, 1)
            nc.gpsimd.memset(causal[:], 0.0).then_inc(cleared, 1)
            nc.gpsimd.memset(half_neg[:], -0.5)
            for n in range(2):
                nc.gpsimd.memset(values[n][:, :, :, HD:32], 0.0).then_inc(cleared, 1)
            pool.wait_ge(cleared, 8)
            for m in (ident, ident_bf):
                nc.gpsimd.affine_select(out=m[:], in_=m[:], pattern=[[-1, P]], compare_op=ALU.not_equal, fill=1.0,
                                        base=0, channel_multiplier=1).then_inc(consts, 1)
            nc.gpsimd.affine_select(out=causal[:], in_=causal[:], pattern=[[-1, P]], compare_op=ALU.is_ge,
                                    fill=MASKED, base=0, channel_multiplier=1).then_inc(consts, 1)
            for n in range(2):
                nc.gpsimd.memset(values[n][:, :, :, HD:HD + 1], 1.0).then_inc(consts, 1)
            split_x(0)
            for n, stage in enumerate(PROLOGUE[:-1]):
                misc_stage(-1, 0, stage, n + 1)
            split_x(1)
            misc_stage(-1, 3, "m", len(PROLOGUE))
            iteration(0, 0)
            by_two(pool, iteration, 1, LAST - 1)
            iteration(LAST, LAST % 2)
            for n, stage in enumerate(EPILOGUE):
                misc_stage(B, 0, stage, FILLS_BEFORE_EPILOGUE + n + 1)
                if stage == "p1":
                    inverse_std(ln_step, rstd_step, LAST)

            def low(T, tpar):
                pool.wait_ge(h_hi_done, T + 1)
                nc.gpsimd.tensor_tensor(h_lo[tpar][:], hidden[tpar][:], h_hi[tpar][:].bitcast(fp32),
                                        ALU.subtract).then_inc(h_lo_done, 1)

            def chunk(c, par):
                first = isinstance(c, int) and c == 0
                for t in range(HT):
                    low(HT * c + t, (par + t) % 2)
                    if not first and t == 5:
                        inverse_std(ln2_step, rstd2_step, c - 1)

            chunk(0, 0)
            by_two(pool, chunk, 1, LAST - 1)
            chunk(LAST, LAST % 2)
            inverse_std(ln2_step, rstd2_step, LAST)




def laid_out(i):
    f = {k: np.asarray(v) for k, v in i.items()}
    x = f["L0_attn_x"]
    wqkv = f["L0_attn_w_qkv"].reshape(KD, P, 3, HEADS // 2, 2, HD)
    wqk = wqkv[:, :, 0:2].transpose(1, 0, 2, 4, 5, 3).reshape(P, KD * 4 * P)
    wv = f["L0_attn_w_qkv"].reshape(KD, P, 3, D)[:, :, 2].transpose(1, 0, 2).reshape(P, KD * D)
    hidden = HT * P

    def rows(routed, shared):
        a = np.zeros((hidden, routed.shape[-1]), routed.dtype)
        a[:E * H] = routed.reshape(E * H, -1)
        a[E * H:E * H + HS] = shared
        return a

    w1 = rows(f["L0_ffn_w1"], f["L0_ffn_ws1"])
    w3 = rows(f["L0_ffn_w3"], f["L0_ffn_ws3"])
    w2 = rows(f["L0_ffn_w2"].transpose(0, 2, 1), f["L0_ffn_ws2"].T)
    up = [w.reshape(HT, P, KD, P).transpose(0, 3, 2, 1) for w in (w1, w3)]
    wt = np.concatenate([*up, w2.reshape(HT, P, KD, P)], axis=2)
    b13 = np.stack([rows(f["L0_ffn_b1"].reshape(E, H, 1), f["L0_ffn_bs1"][:, None]),
                    rows(f["L0_ffn_b3"].reshape(E, H, 1), f["L0_ffn_bs3"][:, None])])
    b13 = b13.reshape(2, HT, P).transpose(2, 0, 1)
    b2 = np.concatenate([f["L0_ffn_b2"], f["L0_ffn_b2"], f["L0_ffn_bs2"][None]])
    return {
        "xT": np.concatenate([x, x[:1]]).reshape(B + 1, S, KD, P).transpose(0, 3, 2, 1),
        "x": x.reshape(B, QT, P, D).transpose(0, 2, 1, 3),
        "wqk": wqk,
        "wv": wv,
        "wo": f["L0_attn_w_out"].reshape(KD, P, D).transpose(1, 0, 2).reshape(P, KD * D),
        "gw": f["L0_ffn_gate_w"].T.reshape(KD, P, E).transpose(1, 0, 2),
        "gb": np.broadcast_to(f["L0_ffn_gate_b"], (P, E)),
        "wt": wt,
        "b13": b13,
        "b2": b2,
    }


def kernel(**inputs):
    import concourse.bacc as bacc
    from concourse.bass_utils import run_bass_kernel_spmd as run

    nc = bacc.Bacc("TRN2", target_bir_lowering=False, num_devices=1)
    arrays, args = {}, {}
    for name, a in laid_out(inputs).items():
        a = np.ascontiguousarray(a)
        arrays[f"in_{name}"] = a
        args[name] = nc.dram_tensor(f"in_{name}", a.shape, mybir.dt.from_np(a.dtype), kind="ExternalInput").ap()
    args["out"] = nc.dram_tensor("out_0", (B, P, QT, D), mybir.dt.float32, kind="ExternalOutput").ap()
    postln_layer(nc, **args)
    got = run(nc, [arrays], core_ids=[0]).results[0]["out_0"]
    return np.ascontiguousarray(got.transpose(0, 2, 1, 3)).reshape(B, S, D)
```

```python
from contextlib import ExitStack

import numpy as np

import concourse.bass as bass
from concourse import mybir

P = 128
B, S, D = 8, 512, 256
HEADS, HD = 16, 16
E, H, HS, TOP_K = 16, 176, 352, 6
KD = D // P
QT = S // P
GH = 4
NG = HEADS // GH
SUBS = 8
STACK = 6 * HD
SHIFT_ROWS = 3
Q_BLOCKS = (0, 0, 0, 1, 1, 2)
K_BLOCKS = (0, 1, 2, 0, 1, 0)
FILLS = 11
HT = -(-(E * H + HS) // P)
HT_ROUTED = E * H // P
EPS = 1e-5
MASKED = -1e30
TAKEN = -3.0e38
TWO_ONES = float(np.array([0x3F803F80], np.uint32).view(np.float32)[0])
ABOVE_ALL = 3.3e38

SCORE_FILLS = (
    [(3, (h,)) for h in range(4)] + [(2, (h,)) for h in range(4)] + [(1, (0, 1)), (1, (2, 3)), (0, (0, 1, 2, 3))]
)
FILLS_OF_SUB = [(0, 1), (2,), (3, 4), (5,), (6,), (7,), (8, 9), (10,)]

MISC = {
    (0, 0): "q0", (0, 1): "q1", (0, 2): "m", (0, 3): "k0", (0, 4): "k1", (0, 6): "v0", (0, 7): "v1",
    (1, 0): "t0", (1, 1): "t1", (1, 2): "m", (1, 4): "p0", (1, 6): "p1",
    (2, 2): "m", (2, 4): "x0", (2, 5): "x1",
    (3, 0): "r", (3, 2): "m", (3, 7): "c",
}
REST_AT = {(0, 1): 0, (0, 2): 1, (0, 4): 2, (0, 5): 3}
PARTS_AT = {(0, 2): 0, (0, 3): 1, (0, 5): 2, (0, 6): 3}
SUM_AT = {(1, 5): 0, (1, 7): 1}
STATS_AT = {(1, 6): 0, (2, 0): 1}
NORMALIZE_AT = {(2, 2): 0, (2, 3): 1}
ROUTE_AT = {(3, 1): 0, (3, 3): 1, (3, 4): 2, (3, 5): 3, (3, 6): 4}
ATTEND_AT = {1: 1, 2: 2, 3: 3}
SHIFT_AT = {(0, 3): 0, (0, 4): 1, (1, 3): 0, (1, 4): 1, (2, 3): 0, (2, 4): 1, (3, 3): 0, (3, 4): 1}
SPLIT_X_AT = (2, 7)
SOFTMAX_AT = (3, 3)
INVERSE_AT = (2, 1)
READ_AT, ROWS_AT, RECIP_AT, NORM_AT, ATTEND_FIRST_AT = 3, 5, 5, 6, 7
NEXT_BATCH = ("q0", "q1", "k0", "k1", "v0", "v1")
QK = NEXT_BATCH[:4]
BATCH_BEFORE = ("t0", "t1", "p0", "p1", "x0", "x1", "r", "c")
PROLOGUE = ["q0", "q1", "k0", "k1", "v0", "v1", "m"]
EPILOGUE = list(BATCH_BEFORE)
ROWS_TILE = 1
FIRST_W_AT = {(3, 4): 0, (3, 5): 1}
EPILOGUE_AT = {2: "t0", 3: "t1", 4: "p0", 5: "p1", 7: "x0", 8: "x1", 9: "r", 11: "c"}
INVERSE_TILE, NORMALIZE_TILE, SOFTMAX_TILE, STORE_X1_TILE, STORE_C_TILE = 5, 6, 10, 11, 12
W_AFTER_A = 16


def key_of(stage, g=None):
    return [k for k in MISC if MISC[k] == stage and g in (None, k[0])][0]


def has(b, g, stage):
    first, last = isinstance(b, int) and b == 0, isinstance(b, int) and b == B - 1
    if first and stage in BATCH_BEFORE:
        return False
    return not (last and (stage in NEXT_BATCH or (stage == "m" and g == NG - 1)))


MISC_FIRST = [k for k in MISC if has(0, k[0], MISC[k])]


def fill_no(b, key):
    if isinstance(b, int) and b == 0:
        return len(PROLOGUE) + MISC_FIRST.index(key) + 1
    keys = list(MISC)
    if isinstance(b, int) and b == B - 1:
        keys = [k for k in keys if has(b, k[0], MISC[k])]
    return (b - 1) * len(MISC) + (len(PROLOGUE) + len(MISC_FIRST) + keys.index(key) + 1)


FILLS_BEFORE_EPILOGUE = (
    len(PROLOGUE) + len(MISC_FIRST) + (B - 2) * len(MISC) + len([k for k in MISC if has(B - 1, k[0], MISC[k])])
)


def postln_layer(nc, xT, x, wqk, wv, wo, gw, gb, wt, b13, b2, out):
    fp32, f32r, bf16 = mybir.dt.float32, mybir.dt.float32r, mybir.dt.bfloat16
    ALU, ACT, AX = mybir.AluOpType, mybir.ActivationFunctionType, mybir.AxisListType

    ctx = ExitStack()
    phase_a = ExitStack()

    def sem(name):
        return ctx.enter_context(nc.semaphore(name))

    def sb(name, shape, dt=fp32, where=ctx):
        return where.enter_context(nc.sbuf_tensor(name, shape, dt))

    def sa(name, shape, dt=fp32):
        return sb(name, shape, dt, phase_a)

    with ctx:
        x1_d = nc.dram_tensor("x1_d", (B, P, QT, D), fp32).ap()
        x1T_d = nc.dram_tensor("x1T_d", (B, 2, P, KD, S), fp32).ap()
        c_d = nc.dram_tensor("c_d", (3, E, B, S), fp32).ap()

        ident = sb("ident", [P, P])
        half_neg = sb("half_neg", [P, QT])
        stats = sb("stats", [P, QT, 6])
        mean_var = sb("mean_var", [P, QT, 2])
        var_eps = sb("var_eps", [P, QT])
        rstd = sb("rstd", [P, QT])

        stack_q, stack_k = [None, None], [None, None]
        stack_q[0] = sa("stack_q0", [P, HEADS, S], bf16)
        stack_k[0] = sa("stack_k0", [P, HEADS, S], bf16)
        parts = [[sa(f"{n}_{p}", [P, 2, S], bf16) for p in ("h", "m", "l")] for n in ("q", "k")]
        rest = sa("rest", [P, 2, S])
        xT_raw = sa("xT_raw", [P, KD, S])
        XT = [sa(f"xT_{n}", [P, KD, S], f32r) for n in ("hi", "lo")]
        WQK = [sa(f"wqk_{n}", [P, KD, 4, P], f32r) for n in ("hi", "lo")]
        WV = [sa(f"wv_{n}", [P, KD, D], f32r) for n in ("hi", "lo")]
        stack_q[1] = sa("stack_q1", [P, HEADS, S], bf16)
        stack_k[1] = sa("stack_k1", [P, HEADS, S], bf16)
        probs = [sa(f"probs{kt}", [P, GH, S - P * kt]) for kt in range(QT)]
        values = [sa(f"values{n}", [P, QT, HEADS, 32]) for n in range(2)]
        ident_bf = sa("ident_bf", [P, P], bf16)
        causal = sa("causal", [P, P], bf16)
        shift = sa("shift", [E, P])
        shift_rest = sa("shift_rest", [E, P])
        shift_parts = [[sa(f"shift_{p}{n}", [E, P], bf16) for p in ("h", "m", "l")] for n in range(2)]
        rowmax = [sa(f"rowmax{n}", [P, GH, QT]) for n in range(2)]
        attn_T = sa("attn_T", [P, S])
        attn = sa("attn", [P, QT, D])
        recip = sa("recip", [P, QT, GH])
        WO = [sa(f"wo_{n}", [P, KD, D], f32r) for n in ("hi", "lo")]
        GW = sa("gw_hi_lo", [P, KD, 2 * E], f32r)
        gw_raw = sa("gw_raw", [P, KD, E])
        gate_b = sa("gate_b", [P, E])
        x_res = sa("x_res", [P, QT, D])
        t_raw = sa("t_raw", [P, KD, S])
        t_hi = sa("t_hi", [P, KD, S], f32r)
        t_lo = sa("t_lo", [P, KD, S], f32r)
        x1 = sa("x1", [P, QT, D])
        logit_lo = sa("logit_lo", [P, QT, E])
        logits = sa("logits", [P, QT, E])
        top = sa("top", [P, QT])
        expo = sa("expo", [P, QT, E])
        total = sa("total", [P, QT])
        gate = sa("gate", [P, QT, E])
        biased = sa("biased", [P, QT, E + 2])
        top8 = sa("top8", [P, QT, 8])
        marked = sa("marked", [P, QT, E + 2])
        weight = sa("weight", [P, QT, E])
        cT_raw = sa("cT_raw", [E, S])
        cT_hi = sa("cT_hi", [E, S], f32r)
        cT_lo = sa("cT_lo", [E, S], f32r)
        raw0 = probs[0][:].rearrange("p h t -> p (h t)")
        wqk_raw, wv_raw, wo_raw = raw0[:, 0:1024], raw0[:, 1024:1536], raw0[:, 1536:2048]
        phase_a.close()

        w_raw = [sb(f"w_raw{n}", [P, 6, P]) for n in range(2)]
        X1T = [sb("x1T_0", [P, 2, KD, S], f32r)]
        CT = [sb(f"cT_{n}", [2 * E + 1, S], f32r) for n in range(2)]
        bias = sb("bias13", [P, 2, HT])
        B2 = [sb(f"b2_{n}", [2 * E + 1, D], f32r) for n in ("hi", "lo")]
        c_all = [sb(f"c_all{n}", [P, S]) for n in range(2)]
        gated = [sb(f"gated{n}", [P, S]) for n in range(2)]
        hidden = [sb(f"hidden{n}", [P, S]) for n in range(2)]
        b2_raw = hidden[1][0:2 * E + 1, 0:D]
        h_hi = [sb(f"h_hi{n}", [P, S], f32r) for n in range(2)]
        h_lo = [sb(f"h_lo{n}", [P, S], f32r) for n in range(2)]
        w_all = sb("w_hi_lo", [P, HT, 2, 6, P], f32r)
        W = [w_all[:, :, n] for n in range(2)]
        X1T.append(sb("x1T_1", [P, 2, KD, S], f32r))
        y_T = sb("y_T", [P, KD, S])
        x1_b = sb("x1_b", [P, QT, D])

        psum = ctx.enter_context(nc.psum_tensor("psum", [P, 8, S], fp32))
        st = [psum[:, 2 * n:2 * n + 2, :] for n in range(2)]
        sm = [psum[:, 4 + n, :] for n in range(2)]
        ov = psum[:, 6, :]
        misc = psum[:, 7, :]
        PROLOGUE_BANKS = [psum[:, n, :] for n in (0, 1, 2, 3, 6, 7)]
        u_ps = [psum[:, n, :] for n in range(2)]
        v_ps = [psum[:, 2 + n, :] for n in range(2)]
        y_ps = [psum[:, 4 + n, :] for n in range(2)]
        tr_ps = [psum[:, 6 + n, :] for n in range(2)]

        w_loaded = sem("w_loaded")
        gw_loaded = sem("gw_loaded")
        xT_loaded = sem("xT_loaded")
        xres_loaded = sem("xres_loaded")
        cleared = sem("cleared")
        ones_set = sem("ones_set")
        consts = sem("consts")
        w_hi_done = sem("w_hi_done")
        w_lo_done = sem("w_lo_done")
        xT_hi_done = sem("xT_hi_done")
        xT_lo_done = sem("xT_lo_done")
        misc_full = sem("misc_full")
        misc_free = sem("misc_free")
        rest_done = sem("rest_done")
        part_m_done = sem("part_m_done")
        part_l_done = sem("part_l_done")
        stack_loaded = sem("stack_loaded")
        sm_full = sem("sm_full")
        sm_free = sem("sm_free")
        shift_step = sem("shift_step")
        shift_loaded = sem("shift_loaded")
        st_full = sem("st_full")
        exp_done = sem("exp_done")
        mask_done = sem("mask_done")
        pv_done = sem("pv_done")
        attn_T_done = sem("attn_T_done")
        rows_full = sem("rows_full")
        rows_used = sem("rows_used")
        recip_done = sem("recip_done")
        t_lo_done = sem("t_lo_done")
        ln_step = sem("ln_step")
        rstd_step = sem("rstd_step")
        x1_done = sem("x1_done")
        x1_stored = sem("x1_stored")
        tail_free = sem("tail_free")
        router_step = sem("router_step")
        router_exp = sem("router_exp")
        cT_lo_done = sem("cT_lo_done")
        c_stored = sem("c_stored")
        passed_dve = sem("passed_dve")
        passed_pool = sem("passed_pool")
        passed_sp = sem("passed_sp")
        wt_loaded = [sem(f"wt_loaded{n}") for n in range(2)]
        small_loaded = sem("small_loaded")
        b2_step = sem("b2_step")
        wt_hi = sem("wt_hi")
        wt_lo = sem("wt_lo")
        x1T_loaded = [sem(f"x1T_loaded{n}") for n in range(2)]
        x1b_loaded = sem("x1b_loaded")
        c_all_loaded = [sem(f"c_all_loaded{n}") for n in range(2)]
        u_full = sem("u_full")
        v_full = sem("v_full")
        gated_done = sem("gated_done")
        v_used = sem("v_used")
        hidden_done = sem("hidden_done")
        h_hi_done = sem("h_hi_done")
        h_lo_done = sem("h_lo_done")
        down_done = sem("down_done")
        y_T_done = sem("y_T_done")
        tr_full = sem("tr_full")
        y_sum = sem("y_sum")
        ln2_step = sem("ln2_step")
        rstd2_step = sem("rstd2_step")
        y_done = sem("y_done")
        out_stored = sem("out_stored")

        block = ctx.enter_context(nc.Block())
        PARTS3 = ((0, 0), (0, 1), (1, 0))
        LAST = B - 1
        STEPS_R = 10

        def settle(eng, passed):
            eng.sem_inc(passed, 1)

        def by_two(eng, body, first, second_last):
            with eng.Fori(0, (second_last - first + 1) // 2) as turn:
                for k in range(2):
                    body(2 * turn + (first + k), (first + k) % 2)

        @block.sync
        def _(sp):
            sp.dma_start(xT_raw[:], xT[0]).then_inc(xT_loaded, 16)
            sp.dma_start(wqk_raw, wqk).then_inc(w_loaded, 16)
            sp.dma_start(wv_raw, wv).then_inc(w_loaded, 16)
            sp.dma_start(wo_raw, wo).then_inc(w_loaded, 16)
            sp.dma_start(gw_raw[:], gw).then_inc(gw_loaded, 16)
            sp.dma_start(gate_b[:], gb).then_inc(gw_loaded, 16)

            def load_stack(nb, par):
                for n, (dst, blocks) in enumerate(((stack_q[par], Q_BLOCKS), (stack_k[par], K_BLOCKS))):
                    sp.wait_ge(part_l_done, 4 * nb + (2 * n + 2))
                    for j, part in enumerate(blocks):
                        sp.dma_start(dst[HD * j:HD * j + HD, :, :], parts[n][part][:]).then_inc(stack_loaded, 16)

            def load_shift(G, par, gpar, g):
                sp.wait_ge(shift_step, 4 * G + 4)
                for j in range(SHIFT_ROWS):
                    sp.dma_start(
                        stack_q[par][STACK + j:STACK + j + 1, GH * g:GH * g + GH, :], shift_parts[gpar][j][:]
                    ).then_inc(shift_loaded, 16)

            def iteration(b, par):
                last = isinstance(b, int) and b == LAST
                first = isinstance(b, int) and b == 0
                if not last:
                    sp.wait_ge(xT_lo_done, b + 2)
                    sp.dma_start(xT_raw[:], xT[b + 2]).then_inc(xT_loaded, 16)
                load_shift(4 * b + 1, par, 1, 1)
                if not last:
                    if not first:
                        sp.wait_ge(st_full, 8 * 4 * b)
                    load_stack(b + 1, 1 - par)
                load_shift(4 * b + 2, par, 0, 2)
                if not first:
                    sp.wait_ge(x1_done, 2 * b)
                sp.dma_start(x_res[:], x[b]).then_inc(xres_loaded, 16)
                load_shift(4 * b + 3, par, 1, 3)
                if last:
                    load_first_chunk()
                if not first:
                    store_x1(b - 1)
                if not last:
                    load_shift(4 * b + 4, 1 - par, 0, 0)
                if not first:
                    store_c(b - 1)
                    sp.wait_ge(x1_stored, 48 * b)
                    sp.wait_ge(c_stored, 48 * b)
                    sp.sem_inc(tail_free, 1)

            def store_x1(t):
                sp.wait_ge(t_lo_done, 4 * t + 4)
                sp.dma_start(x1_d[t], x1[:]).then_inc(x1_stored, 16)
                sp.dma_start(x1T_d[t, 0], t_hi[:].bitcast(fp32)).then_inc(x1_stored, 16)
                sp.dma_start(x1T_d[t, 1], t_lo[:].bitcast(fp32)).then_inc(x1_stored, 16)

            def store_c(t):
                sp.wait_ge(cT_lo_done, t + 1)
                sp.dma_start(c_d[0, :, t, :], cT_raw[:]).then_inc(c_stored, 16)
                sp.dma_start(c_d[1, :, t, :], cT_hi[:].bitcast(fp32)).then_inc(c_stored, 16)
                sp.dma_start(c_d[2, :, t, :], cT_lo[:].bitcast(fp32)).then_inc(c_stored, 16)

            def load_w(t):
                if t >= 2:
                    sp.wait_ge(wt_lo, t - 1)
                sp.dma_start(w_raw[t % 2][:], wt[t]).then_inc(wt_loaded[t % 2], 16)

            def load_chunk(c, par):
                sp.dma_start(X1T[par][:].bitcast(fp32), x1T_d[c].rearrange("n p k t -> p n k t")).then_inc(
                    x1T_loaded[par], 16)
                sp.dma_start(CT[par][0:E, :].bitcast(fp32), c_d[1, :, c, :]).then_inc(x1T_loaded[par], 16)
                sp.dma_start(CT[par][E:2 * E, :].bitcast(fp32), c_d[2, :, c, :]).then_inc(x1T_loaded[par], 16)

            def load_c_all(T, c, t, tpar):
                if not (isinstance(T, int) and T < 2):
                    sp.wait_ge(hidden_done, T - 1)
                    settle(sp, passed_sp)
                first_e, last_e = t * P // H, (t * P + P - 1) // H
                edge = last_e * H - t * P if last_e > first_e else P // 2
                for e, lo, hi in ((first_e, 0, edge), (last_e, edge, P)):
                    sp.dma_start(c_all[tpar][lo:hi, :], c_d[0, e, c, :].partition_broadcast(hi - lo)).then_inc(
                        c_all_loaded[tpar], 16)

            def chunk(c, par):
                whole = isinstance(c, int)
                for t in range(HT_ROUTED):
                    if whole and c == 0 and t + 2 < HT:
                        load_w(t + 2)
                    load_c_all(HT * c + t, c, t, (par + t) % 2)
                    if whole and c == 0 and t == STORE_X1_TILE:
                        store_x1(LAST)
                    if whole and c == 0 and t == STORE_C_TILE:
                        store_c(LAST)
                    if t == 4 and not (whole and c == LAST):
                        if not (whole and c == 0):
                            sp.wait_ge(y_T_done, 2 * c)
                        load_chunk(c + 1, 1 - par)
                    if t == 9:
                        if not (whole and c == 0):
                            sp.wait_ge(y_done, c)
                            store_out(c - 1)
                            sp.wait_ge(out_stored, 16 * c)
                        sp.dma_start(x1_b[:], x1_d[c]).then_inc(x1b_loaded, 16)
                for t in range(HT_ROUTED, HT - 2):
                    if whole and c == 0:
                        load_w(t + 2)

            def store_out(c):
                sp.dma_start(out[c], x1_b[:]).then_inc(out_stored, 16)

            def load_first_chunk():
                sp.wait_ge(part_l_done, 4 * B)
                sp.wait_ge(stack_loaded, 192 * B)
                sp.wait_ge(xT_lo_done, B + 1)
                sp.wait_ge(st_full, 8 * NG * LAST + 1)
                load_w(0)
                load_w(1)
                sp.dma_start(bias[:], b13).then_inc(small_loaded, 16)
                sp.dma_start(b2_raw, b2).then_inc(small_loaded, 16)
                load_chunk(0, 0)

            sp.sem_inc(tail_free, 1)
            for n, (dst, blocks) in enumerate(((stack_q[0], Q_BLOCKS), (stack_k[0], K_BLOCKS))):
                for part, ready in enumerate((misc_free, part_m_done, part_l_done)):
                    sp.wait_ge(ready, 2 * n + 2)
                    for j in range(6):
                        if blocks[j] == part:
                            sp.dma_start(dst[HD * j:HD * j + HD, :, :], parts[n][part][:]).then_inc(
                                stack_loaded, 16)
            sp.wait_ge(xT_lo_done, 1)
            sp.dma_start(xT_raw[:], xT[1]).then_inc(xT_loaded, 16)
            load_shift(0, 0, 0, 0)
            iteration(0, 0)
            by_two(sp, iteration, 1, LAST - 1)
            iteration(LAST, LAST % 2)
            chunk(0, 0)
            sp.wait_ge(x1_stored, 48 * B)
            sp.wait_ge(c_stored, 48 * B)
            by_two(sp, chunk, 1, LAST - 1)
            chunk(LAST, LAST % 2)
            sp.wait_ge(y_done, B)
            store_out(LAST)
            sp.wait_ge(out_stored, 16 * B)

        @block.tensor
        def _(pe):
            def fill(n):
                if not (isinstance(n, int) and n == 1):
                    pe.wait_ge(misc_free, n - 1)

            def three_pass(dst, lhs, rhs):
                n = 0
                for k in range(KD):
                    for a, b in PARTS3:
                        last = nc.tensor.matmul(dst, lhs(a, k), rhs(b, k), start=n == 0, stop=n == 3 * KD - 1)
                        n += 1
                return last

            def scores_for_max(G, par, g, f):
                n = FILLS * G + f
                bank = (g + f) % 2
                if not (isinstance(n, int) and n < 2):
                    pe.wait_ge(sm_free, n - 1)
                qt, heads = SCORE_FILLS[f]
                width = P * (qt + 1)
                for i, h in enumerate(heads):
                    head = GH * g + h
                    dst = sm[bank][:, i * width:(i + 1) * width]
                    nc.tensor.matmul(dst, stack_q[par][0:STACK, head, qt * P:qt * P + P],
                                     stack_k[par][0:STACK, head, 0:width], start=True, stop=False)
                    last = nc.tensor.matmul(dst[:, width - P:width], ident_bf[:], causal[:], start=False, stop=True)
                last.then_inc(sm_full, 1)

            def scores(G, par, g, s):
                kt, pair = s // 2, s % 2
                n = 8 * G + s
                if not (isinstance(n, int) and n < 2):
                    pe.wait_ge(exp_done, n - 1)
                for i in range(2):
                    head = GH * g + 2 * pair + i
                    last = nc.tensor.matmul(st[s % 2][:, i, 0:S - kt * P],
                                            stack_k[par][0:STACK + SHIFT_ROWS, head, kt * P:kt * P + P],
                                            stack_q[par][0:STACK + SHIFT_ROWS, head, kt * P:S],
                                            start=True, stop=True)
                last.then_inc(st_full, 1)

            def attend(G, par, g, kt):
                if kt == 0 and not (isinstance(G, int) and G == 0):
                    pe.wait_ge(rows_used, G)
                pe.wait_ge(mask_done, 4 * G + (kt + 1))
                for j in range(GH):
                    last = nc.tensor.matmul(ov[32 * j:32 * j + 32, kt * P:S], values[par][:, kt, GH * g + j, :],
                                            probs[kt][:, j, :], start=kt == 0, stop=kt == QT - 1,
                                            skip_group_check=True)
                last.then_inc(pv_done, 1)

            def project_qk(nb, tile):
                if tile == 0:
                    pe.wait_ge(xT_lo_done, nb + 1)
                dst = PROLOGUE_BANKS[tile] if isinstance(nb, int) and nb == 0 else misc
                three_pass(dst, lambda a, k: WQK[a][:, k, tile, :], lambda b, k: XT[b][:, k, :]).then_inc(
                    misc_full, 1)

            def project_v(nb, f):
                dst = PROLOGUE_BANKS[4 + f] if isinstance(nb, int) and nb == 0 else misc
                for j in range(2):
                    qt = 2 * f + j
                    last = three_pass(dst[:, j * D:j * D + D], lambda a, k: XT[a][:, k, qt * P:qt * P + P],
                                      lambda b, k: WV[b][:, k, :])
                last.then_inc(misc_full, 1)

            def transpose_max(G, gpar):
                pe.wait_ge(sm_free, FILLS * G + FILLS)
                nc.tensor.transpose(misc[0:E, 0:P], rowmax[gpar][:].rearrange("p h q -> p (h q)"), ident[:]).then_inc(
                    misc_full, 1)

            def transpose_out(G):
                pe.wait_ge(attn_T_done, G + 1)
                for qt in range(QT):
                    last = nc.tensor.transpose(ov[:, qt * P:qt * P + P], attn_T[:, qt * P:qt * P + P], ident[:])
                last.then_inc(rows_full, 1)

            def transpose_rows(src, k):
                for qt in range(QT):
                    last = nc.tensor.transpose(misc[:, qt * P:qt * P + P], src[:, qt, k * P:k * P + P], ident[:])
                last.then_inc(misc_full, 1)

            def project_out(t, f):
                pe.wait_ge(t_lo_done, 4 * t + 2)
                for j in range(2):
                    qt = 2 * f + j
                    last = three_pass(misc[:, j * D:j * D + D],
                                      lambda a, k: (t_hi, t_lo)[a][:, k, qt * P:qt * P + P],
                                      lambda b, k: WO[b][:, k, :])
                last.then_inc(misc_full, 1)

            def route(t):
                pe.wait_ge(t_lo_done, 4 * t + 4)
                for qt in range(QT):
                    dst = misc[:, 2 * E * qt:2 * E * qt + 2 * E]
                    for k in range(KD):
                        nc.tensor.matmul(dst, t_hi[:, k, qt * P:qt * P + P], GW[:, k, :], start=k == 0, stop=False)
                    for k in range(KD):
                        last = nc.tensor.matmul(dst[:, 0:E], t_lo[:, k, qt * P:qt * P + P], GW[:, k, 0:E],
                                                start=False, stop=k == KD - 1)
                last.then_inc(misc_full, 1)

            def transpose_weights(t):
                pe.wait_ge(router_step, STEPS_R * (t + 1))
                for qt in range(QT):
                    last = nc.tensor.transpose(misc[0:E, qt * P:qt * P + P], weight[:, qt, :], ident[:])
                last.then_inc(misc_full, 1)

            def misc_stage(b, g, stage):
                if stage in QK:
                    project_qk(b + 1, QK.index(stage))
                elif stage[0] == "v":
                    project_v(b + 1, int(stage[1]))
                elif stage == "m":
                    transpose_max(4 * b + (g + 1), (g + 1) % 2)
                elif stage[0] == "t":
                    if stage == "t0":
                        pe.wait_ge(rows_used, NG * b)
                    transpose_rows(attn, int(stage[1]))
                elif stage[0] == "p":
                    project_out(b - 1, int(stage[1]))
                elif stage[0] == "x":
                    if stage == "x0":
                        pe.wait_ge(x1_done, 2 * b)
                    transpose_rows(x1, int(stage[1]))
                elif stage == "r":
                    route(b - 1)
                else:
                    transpose_weights(b - 1)

            def iteration(b, par):
                whole = isinstance(b, int)
                for g in range(NG):
                    G = 4 * b + g
                    pe.wait_ge(stack_loaded, 192 * (b + 1))
                    pe.wait_ge(shift_loaded, 48 * (G + 1))
                    for s in range(SUBS):
                        scores(G, par, g, s)
                        if not (whole and 4 * b + g + 2 >= NG * B):
                            if g == 2 and s == 0:
                                pe.wait_ge(stack_loaded, 192 * (b + 2))
                            for f in FILLS_OF_SUB[s]:
                                scores_for_max(G + 2, par if g < 2 else 1 - par, (g + 2) % NG, f)
                        if not (whole and b == 0 and g == 0):
                            if s in ATTEND_AT:
                                attend(G - 1, par if g else 1 - par, (g - 1) % NG, ATTEND_AT[s])
                            if s == ROWS_AT:
                                transpose_out(G - 1)
                        if s == ATTEND_FIRST_AT:
                            attend(G, par, g, 0)
                        stage = MISC.get((g, s))
                        if stage and has(b, g, stage):
                            fill(fill_no(b, (g, s)))
                            misc_stage(b, g, stage)

            pe.wait_ge(consts, 5)
            for n, stage in enumerate(PROLOGUE[:-1]):
                if stage in ("q0", "v0"):
                    pe.wait_ge(w_hi_done, 1 if stage == "q0" else 2)
                    pe.wait_ge(w_lo_done, 1 if stage == "q0" else 2)
                misc_stage(-1, 3, stage)
            pe.wait_ge(stack_loaded, 192)
            for G in range(2):
                for f in range(FILLS):
                    scores_for_max(G, 0, G, f)
                    if (G, f) == (1, 1):
                        fill(len(PROLOGUE))
                        transpose_max(0, 0)
            pe.wait_ge(ones_set, 2)
            pe.wait_ge(w_lo_done, 4)
            iteration(0, 0)
            by_two(pe, iteration, 1, LAST - 1)
            iteration(LAST, LAST % 2)

            def epilogue(t):
                if t == 0:
                    for kt in (1, 2, 3):
                        attend(NG * B - 1, LAST % 2, NG - 1, kt)
                if t == ROWS_TILE:
                    transpose_out(NG * B - 1)
                if t in EPILOGUE_AT:
                    fill(FILLS_BEFORE_EPILOGUE + EPILOGUE.index(EPILOGUE_AT[t]) + 1)
                    misc_stage(B, 0, EPILOGUE_AT[t])

            def up(T, t, par, tpar):
                for ps, full, used, first in ((u_ps, u_full, gated_done, 0), (v_ps, v_full, v_used, 2)):
                    if not (isinstance(T, int) and T < 2):
                        pe.wait_ge(used, T - 1)
                    three_pass(ps[tpar], lambda a, k: W[a][:, t, first + k, :],
                               lambda b, k: X1T[par][:, b, k, :]).then_inc(full, 1)

            def down(T, t, tpar):
                pe.wait_ge(h_lo_done, T + 1)
                for d in range(KD):
                    for n, (a, b) in enumerate(PARTS3):
                        last = nc.tensor.matmul(y_ps[d], W[a][:, t, 4 + d, :], (h_hi, h_lo)[b][tpar][:],
                                                start=t == 0 and n == 0, stop=False, skip_group_check=True)
                last.then_inc(down_done, 1)

            def down_bias(par):
                for d in range(KD):
                    for a in range(2):
                        last = nc.tensor.matmul(y_ps[d], B2[a][:, d * P:d * P + P], CT[par][:], start=False,
                                                stop=a == 1, skip_group_check=True)
                last.then_inc(down_done, 1)

            def y_rows(c, f):
                if f == 0:
                    pe.wait_ge(y_T_done, 2 * c + 2)
                for j in range(2):
                    for d in range(KD):
                        qt = 2 * f + j
                        last = nc.tensor.transpose(tr_ps[f][:, j * D + d * P:j * D + d * P + P],
                                                   y_T[:, d, qt * P:qt * P + P], ident[:])
                last.then_inc(tr_full, 1)

            def chunk(c, par):
                whole = isinstance(c, int)
                first = whole and c == 0
                for t in range(HT):
                    T = HT * c + t
                    if first:
                        pe.wait_ge(wt_hi, t + 1)
                        pe.wait_ge(wt_lo, t + 1)
                    if t == 0:
                        pe.wait_ge(x1T_loaded[par], (c + (2 - par)) * 24)
                    up(T, t, par, (par + t) % 2)
                    if t >= 2:
                        if t == 2 and not first:
                            pe.wait_ge(y_T_done, 2 * c)
                        down(T - 2, t - 2, (par + t) % 2)
                    elif not first:
                        down(T - 2, HT - 2 + t, (par + t) % 2)
                        if t == 1:
                            pe.wait_ge(b2_step, 3)
                            down_bias(1 - par)
                    if not first and t in (4, 5):
                        y_rows(c - 1, t - 4)
                    if first:
                        epilogue(t)

            pe.wait_ge(exp_done, 8 * NG * B)
            chunk(0, 0)
            by_two(pe, chunk, 1, LAST - 1)
            chunk(LAST, LAST % 2)
            for t in (HT - 2, HT - 1):
                T = HT * LAST + t
                down(T, t, T % 2)
            down_bias(LAST % 2)
            for f in range(2):
                y_rows(LAST, f)

        @block.scalar
        def _(act):
            def copy(dst, src, scale=1.0):
                return nc.scalar.activation(dst, src, ACT.Copy, scale=scale)

            def probabilities(G, s):
                kt, pair = s // 2, s % 2
                act.wait_ge(st_full, 8 * G + (s + 1))
                if not (isinstance(G, int) and G == 0):
                    act.wait_ge(pv_done, 4 * G + (kt - 3))
                nc.scalar.activation(probs[kt][:, 2 * pair:2 * pair + 2, :], st[s % 2][:, :, 0:S - kt * P],
                                     ACT.Exp).then_inc(exp_done, 1)

            def split_w(t):
                if t == W_AFTER_A:
                    act.wait_ge(x1_stored, 48 * B)
                    act.wait_ge(c_stored, 48 * B)
                act.wait_ge(wt_loaded[t % 2], 16 * (t // 2 + 1))
                copy(W[0][:, t], w_raw[t % 2][:]).then_inc(wt_hi, 1)

            def split_x(nb):
                act.wait_ge(xT_loaded, 16 * (nb + 1))
                copy(XT[0][:], xT_raw[:]).then_inc(xT_hi_done, 1)

            shared = misc

            def transposed(k):
                copy(t_hi[:, k, :], misc)
                copy(t_raw[:, k, :], misc).then_inc(misc_free, 1)

            def misc_stage(b, g, stage, n):
                t = b - 1
                if stage in ("p0", "p1", "r"):
                    return
                act.wait_ge(misc_full, n)
                misc = PROLOGUE_BANKS[n - 1] if isinstance(b, int) and b == -1 and stage != "m" else shared
                if stage in QK:
                    tile = QK.index(stage)
                    scale = 0.25 if tile < 2 else 1.0
                    m = 4 * (b + 1) + tile
                    if tile == 0 and not (isinstance(b, int) and b == -1):
                        act.wait_ge(stack_loaded, 192 * (b + 1))
                    if not (isinstance(m, int) and m < 2):
                        act.wait_ge(part_l_done, m - 1)
                    copy(parts[tile // 2][0][:, tile % 2, :], misc, scale)
                    copy(rest[:, tile % 2, :], misc, scale).then_inc(misc_free, 1)
                elif stage[0] == "v":
                    f = int(stage[1])
                    dst = values[(b + 1) % 2 if isinstance(b, int) else g][:, 2 * f:2 * f + 2, :, 0:HD]
                    copy(dst, misc.rearrange("p (q h d) -> p q h d", q=2, h=HEADS)).then_inc(misc_free, 1)
                elif stage == "m":
                    G = 4 * b + (g + 1)
                    if not (isinstance(G, int) and G == 0):
                        act.wait_ge(shift_step, 4 * G)
                    copy(shift[:], misc[0:E, 0:P], -1.0).then_inc(misc_free, 1)
                elif stage[0] == "t":
                    k = int(stage[1])
                    if k == 0:
                        act.wait_ge(tail_free, t + 1)
                    transposed(k)
                elif stage[0] == "x":
                    k = int(stage[1])
                    act.wait_ge(t_lo_done, 4 * t + (k + 1))
                    transposed(k)
                elif stage == "c":
                    copy(cT_hi[:], misc[0:E, :])
                    copy(cT_raw[:], misc[0:E, :]).then_inc(misc_free, 1)

            def middle_part(nb, tile):
                act.wait_ge(rest_done, 4 * nb + (tile + 1))
                copy(parts[tile // 2][1][:, tile % 2, :], rest[:, tile % 2, :]).then_inc(part_m_done, 1)

            def read_attn(G):
                act.wait_ge(pv_done, 4 * G + 4)
                if not (isinstance(G, int) and G == 0):
                    act.wait_ge(recip_done, G)
                copy(attn_T[:], ov).then_inc(attn_T_done, 1)

            def router_softmax(t):
                act.wait_ge(router_step, STEPS_R * t + 3)
                nc.scalar.activation(expo[:], logits[:], ACT.Exp).then_inc(router_exp, 1)

            def iteration(b, par):
                whole = isinstance(b, int)
                for g in range(NG):
                    G = 4 * b + g
                    for s in range(SUBS):
                        probabilities(G, s)
                        if s == READ_AT and not (whole and b == 0 and g == 0):
                            read_attn(G - 1)
                        stage = MISC.get((g, s))
                        if stage and has(b, g, stage):
                            misc_stage(b, 1 - par if stage[0] == "v" else g, stage, fill_no(b, (g, s)))
                        if (g, s) in PARTS_AT and not (whole and b == LAST):
                            middle_part(b + 1, PARTS_AT[g, s])
                        if (g, s) == SOFTMAX_AT and not (whole and b == 0):
                            router_softmax(b - 1)
                        if (g, s) == SPLIT_X_AT and not (whole and b == LAST):
                            split_x(b + 2)
                        if whole and b == LAST and (g, s) in FIRST_W_AT:
                            split_w(FIRST_W_AT[g, s])

            split_x(0)
            act.wait_ge(w_loaded, 48)
            copy(WQK[0][:].rearrange("p k t m -> p (k t m)"), wqk_raw).then_inc(w_hi_done, 1)
            copy(WV[0][:].rearrange("p k n -> p (k n)"), wv_raw).then_inc(w_hi_done, 1)
            copy(WO[0][:].rearrange("p k n -> p (k n)"), wo_raw).then_inc(w_hi_done, 1)
            act.wait_ge(gw_loaded, 32)
            copy(GW[:, :, 0:E], gw_raw[:]).then_inc(w_hi_done, 1)
            for n, stage in enumerate(PROLOGUE[:-1]):
                misc_stage(-1, 0, stage, n + 1)
                if stage in ("q1", "k1"):
                    middle_part(0, n - 1)
                    middle_part(0, n)
            act.wait_ge(misc_full, len(PROLOGUE) - 1)
            split_x(1)
            misc_stage(-1, 3, "m", len(PROLOGUE))
            act.wait_ge(w_lo_done, 4)
            iteration(0, 0)
            by_two(act, iteration, 1, LAST - 1)
            iteration(LAST, LAST % 2)

            def epilogue(t):
                if t == ROWS_TILE - 1:
                    read_attn(NG * B - 1)
                if t == SOFTMAX_TILE:
                    router_softmax(LAST)
                if t in EPILOGUE_AT:
                    misc_stage(B, 0, EPILOGUE_AT[t], FILLS_BEFORE_EPILOGUE + EPILOGUE.index(EPILOGUE_AT[t]) + 1)

            def silu(T, t, tpar):
                act.wait_ge(u_full, T + 1)
                if not (isinstance(T, int) and T < 2):
                    act.wait_ge(v_used, T - 1)
                nc.scalar.activation(gated[tpar][:], u_ps[tpar], ACT.Silu, bias=bias[:, 0, t:t + 1]).then_inc(
                    gated_done, 1)

            def read_y(c):
                act.wait_ge(down_done, (HT + 1) * (c + 1))
                for d in range(KD):
                    copy(y_T[:, d, :], y_ps[d]).then_inc(y_T_done, 1)

            def high(c, t, tpar):
                T = HT * c + t
                act.wait_ge(hidden_done, T + 1)
                if not (isinstance(T, int) and T < 2):
                    act.wait_ge(down_done, (HT + 1) * c + (t - 1 if t >= 2 else t - 2))
                copy(h_hi[tpar][:], hidden[tpar][:]).then_inc(h_hi_done, 1)

            def chunk(c, par):
                first = isinstance(c, int) and c == 0
                for t in range(HT):
                    if t == 2 and not first:
                        read_y(c - 1)
                    if first and t + 2 < HT:
                        split_w(t + 2)
                    silu(HT * c + t, t, (par + t) % 2)
                    if not (first and t == 0):
                        high(c, t - 1, (par + t + 1) % 2)
                    if first:
                        epilogue(t)

            act.wait_ge(small_loaded, 32)
            copy(B2[0][:], b2_raw).then_inc(b2_step, 1)
            chunk(0, 0)
            by_two(act, chunk, 1, LAST - 1)
            chunk(LAST, LAST % 2)
            high(LAST, HT - 1, (LAST + HT - 1) % 2)
            read_y(LAST)

        @block.vector
        def _(dve):
            def split_w(t):
                dve.wait_ge(wt_hi, t + 1)
                nc.vector.tensor_tensor(W[1][:, t], w_raw[t % 2][:], W[0][:, t].bitcast(fp32),
                                        ALU.subtract).then_inc(wt_lo, 1)

            def maxima(G, g, f, gpar):
                qt, heads = SCORE_FILLS[f]
                width, n = P * (qt + 1), len(heads)
                dve.wait_ge(sm_full, FILLS * G + (f + 1))
                src = sm[(g + f) % 2][:, 0:n * width].rearrange("p (h k) -> p h k", h=n)
                nc.vector.reduce_max(rowmax[gpar][:, heads[0]:heads[0] + n, qt], src, AX.X).then_inc(
                    sm_free, 1)

            def layer_norm_stats(src, f, step, base):
                for qt in (2 * f, 2 * f + 1):
                    last = nc.vector.bn_stats(stats[:, qt, :], src[:, qt, :])
                last.then_inc(step, 1)
                dve.wait_ge(step, base + (2 * f + 1))
                settle(dve, passed_dve)
                for qt in (2 * f, 2 * f + 1):
                    last = nc.vector.bn_aggr(mean_var[:, qt, :], stats[:, qt, :])
                last.then_inc(step, 1)

            def normalize(buf, done, tiles=range(QT)):
                for qt in tiles:
                    last = nc.vector.tensor_scalar(buf[:, qt, :], buf[:, qt, :], mean_var[:, qt, 0:1],
                                                   rstd[:, qt:qt + 1], ALU.subtract, ALU.mult)
                last.then_inc(done, 1)

            def misc_stage(b, g, stage, n):
                t = b - 1
                if stage[0] == "p":
                    f = int(stage[1])
                    dve.wait_ge(misc_full, n)
                    if f == 0:
                        dve.wait_ge(xres_loaded, 16 * (t + 1))
                    nc.vector.tensor_tensor(x1[:, 2 * f:2 * f + 2, :],
                                            misc.rearrange("p (q d) -> p q d", q=2),
                                            x_res[:, 2 * f:2 * f + 2, :], ALU.add).then_inc(misc_free, 1)

            def attn_stats(b, f, n):
                dve.wait_ge(misc_free, n)
                layer_norm_stats(x1, f, ln_step, 4 * (b - 1))

            def rest_of(nb, tile, n):
                dve.wait_ge(misc_free, n)
                nc.vector.tensor_tensor(rest[:, tile % 2, :], rest[:, tile % 2, :],
                                        parts[tile // 2][0][:, tile % 2, :], ALU.subtract).then_inc(rest_done, 1)

            def split_shift(G, gpar, n, step):
                high, mid, low = shift_parts[gpar]
                if step == 0:
                    dve.wait_ge(misc_free, n)
                    if not (isinstance(G, int) and G < 2):
                        dve.wait_ge(shift_loaded, 48 * (G - 1))
                    nc.vector.tensor_copy(high[:], shift[:]).then_inc(shift_step, 1)
                elif step == 1:
                    dve.wait_ge(shift_step, 4 * G + 1)
                    nc.vector.tensor_tensor(shift_rest[:], shift[:], high[:], ALU.subtract).then_inc(shift_step, 1)
                elif step == 2:
                    dve.wait_ge(shift_step, 4 * G + 2)
                    nc.vector.tensor_copy(mid[:], shift_rest[:]).then_inc(shift_step, 1)
                else:
                    dve.wait_ge(shift_step, 4 * G + 3)
                    nc.vector.tensor_tensor(low[:], shift_rest[:], mid[:], ALU.subtract).then_inc(shift_step, 1)

            def rows_recip(G):
                dve.wait_ge(rows_full, G + 1)
                rows = ov.rearrange("p (q h c) -> p q h c", q=QT, h=GH)
                nc.vector.reciprocal(recip[:], rows[:, :, :, HD]).then_inc(recip_done, 1)

            def norm_rows(G, g):
                dve.wait_ge(recip_done, G + 1)
                rows = ov.rearrange("p (q h c) -> p q h c", q=QT, h=GH)
                dst = attn[:, :, g * GH * HD:(g + 1) * GH * HD]
                nc.vector.tensor_tensor(dst.rearrange("p q (h d) -> p q h d", h=GH), rows[:, :, :, 0:HD],
                                        recip[:].unsqueeze(3).to_broadcast([P, QT, GH, HD]),
                                        ALU.mult).then_inc(rows_used, 1)

            def route(t, n, part):
                base = STEPS_R * t
                if part == 0:
                    dve.wait_ge(misc_full, n)
                    rows = misc[:, 0:2 * E * QT].rearrange("p (q e) -> p q e", q=QT)
                    nc.vector.tensor_copy(logit_lo[:], rows[:, :, E:2 * E]).then_inc(router_step, 1)
                    dve.wait_ge(router_step, base + 1)
                    nc.vector.tensor_tensor(logits[:], rows[:, :, 0:E], logit_lo[:], ALU.add).then_inc(misc_free, 1)
                elif part == 1:
                    dve.wait_ge(misc_free, n)
                    nc.vector.reduce_max(top[:], logits[:], AX.X).then_inc(router_step, 1)
                    dve.wait_ge(router_step, base + 2)
                    nc.vector.tensor_tensor(logits[:], logits[:], top[:].unsqueeze(2).to_broadcast([P, QT, E]),
                                            ALU.subtract).then_inc(router_step, 1)
                elif part == 2:
                    dve.wait_ge(router_exp, t + 1)
                    nc.vector.reduce_sum(total[:], expo[:], AX.X).then_inc(router_step, 1)
                    dve.wait_ge(router_step, base + 4)
                    nc.vector.reciprocal(total[:], total[:]).then_inc(router_step, 1)
                    dve.wait_ge(router_step, base + 5)
                    nc.vector.tensor_tensor(gate[:], expo[:], total[:].unsqueeze(2).to_broadcast([P, QT, E]),
                                            ALU.mult).then_inc(router_step, 1)
                elif part == 3:
                    dve.wait_ge(router_step, base + 6)
                    nc.vector.tensor_tensor(biased[:, :, 0:E], gate[:],
                                            gate_b[:].unsqueeze(1).to_broadcast([P, QT, E]),
                                            ALU.add).then_inc(router_step, 1)
                    dve.wait_ge(router_step, base + 7)
                    settle(dve, passed_dve)
                    for qt in range(QT):
                        last = nc.vector.max(top8[:, qt, :], biased[:, qt, :])
                    last.then_inc(router_step, 1)
                else:
                    dve.wait_ge(router_step, base + 8)
                    settle(dve, passed_dve)
                    for qt in range(QT):
                        last = nc.vector.match_replace(marked[:, qt, :], top8[:, qt, :], biased[:, qt, :], TAKEN)
                    last.then_inc(router_step, 1)
                    dve.wait_ge(router_step, base + 9)
                    nc.vector.scalar_tensor_tensor(weight[:], marked[:, :, 0:E], TAKEN, gate[:], ALU.is_equal,
                                                   ALU.mult).then_inc(router_step, 1)

            def iteration(b, par):
                whole = isinstance(b, int)
                for g in range(NG):
                    G = 4 * b + g
                    for s in range(SUBS):
                        shifts = has(b, g, "m") and (g, s) in SHIFT_AT
                        first_group = whole and b == 0 and g == 0
                        if shifts:
                            split_shift(G + 1, (g + 1) % 2, fill_no(b, key_of("m", g)), 2 * SHIFT_AT[g, s])
                        if s == NORM_AT and not first_group:
                            norm_rows(G - 1, (g - 1) % NG)
                        if not (whole and 4 * b + g + 2 >= NG * B):
                            for f in FILLS_OF_SUB[s]:
                                maxima(G + 2, (g + 2) % NG, f, g % 2)
                        if shifts:
                            split_shift(G + 1, (g + 1) % 2, fill_no(b, key_of("m", g)), 2 * SHIFT_AT[g, s] + 1)
                        if s == RECIP_AT and not first_group:
                            rows_recip(G - 1)
                        if (g, s) in REST_AT and not (whole and b == LAST):
                            tile = REST_AT[g, s]
                            rest_of(b + 1, tile, fill_no(b, key_of(QK[tile])))
                        if not (whole and b == 0):
                            if (g, s) in SUM_AT:
                                stage = f"p{SUM_AT[g, s]}"
                                misc_stage(b, g, stage, fill_no(b, key_of(stage)))
                            if (g, s) in STATS_AT:
                                f = STATS_AT[g, s]
                                attn_stats(b, f, fill_no(b, key_of(f"p{f}")))
                            if (g, s) in NORMALIZE_AT:
                                f = NORMALIZE_AT[g, s]
                                dve.wait_ge(rstd_step, 2 * b)
                                normalize(x1, x1_done, (2 * f, 2 * f + 1))
                            if (g, s) in ROUTE_AT:
                                route(b - 1, fill_no(b, key_of("r")), ROUTE_AT[g, s])
                        if whole and b == LAST and (g, s) in FIRST_W_AT:
                            split_w(FIRST_W_AT[g, s])

            def epilogue(t):
                if t == ROWS_TILE:
                    rows_recip(NG * B - 1)
                    norm_rows(NG * B - 1, NG - 1)
                stage = EPILOGUE_AT.get(t)
                no = FILLS_BEFORE_EPILOGUE + EPILOGUE.index(stage) + 1 if stage else 0
                if stage in ("p0", "p1"):
                    misc_stage(B, 0, stage, no)
                    attn_stats(B, int(stage[1]), no)
                if t == NORMALIZE_TILE:
                    dve.wait_ge(rstd_step, 2 * B)
                    for f in range(2):
                        normalize(x1, x1_done, (2 * f, 2 * f + 1))
                if stage == "r":
                    for part in range(2):
                        route(LAST, no, part)
                if t == SOFTMAX_TILE:
                    for part in range(2, 5):
                        route(LAST, no, part)

            def ones(n):
                rows = stack_k[n][STACK:STACK + SHIFT_ROWS, :, :].rearrange("p h t -> p (h t)").bitcast(fp32)
                nc.vector.memset(rows, TWO_ONES).then_inc(ones_set, 1)

            nc.vector.memset(biased[:, :, E:E + 2], ABOVE_ALL).then_inc(cleared, 1)
            ones(0)
            for n, ((hi, lo), raw, names) in enumerate(
                    ((WQK, wqk_raw, "p k t m -> p (k t m)"), (WV, wv_raw, "p k n -> p (k n)"),
                     (WO, wo_raw, "p k n -> p (k n)"))):
                dve.wait_ge(w_hi_done, n + 1)
                nc.vector.tensor_tensor(lo[:].rearrange(names), raw, hi[:].bitcast(fp32).rearrange(names),
                                        ALU.subtract).then_inc(w_lo_done, 1)
            dve.wait_ge(w_hi_done, 4)
            nc.vector.tensor_tensor(GW[:, :, E:2 * E], gw_raw[:], GW[:, :, 0:E].bitcast(fp32),
                                    ALU.subtract).then_inc(w_lo_done, 1)
            for tile in range(4):
                rest_of(0, tile, tile + 1)
            ones(1)
            for G in range(2):
                for f in range(FILLS):
                    maxima(G, G, f, G)
                    if G == 1 and f in (2, 3, 4, 5):
                        split_shift(0, 0, len(PROLOGUE), f - 2)
            iteration(0, 0)
            by_two(dve, iteration, 1, LAST - 1)
            iteration(LAST, LAST % 2)

            def hide(c, T, t, tpar):
                dve.wait_ge(gated_done, T + 1)
                dve.wait_ge(v_full, T + 1)
                if not (isinstance(T, int) and T < 2):
                    dve.wait_ge(h_lo_done, T - 1)
                routed = t < HT_ROUTED
                nc.vector.scalar_tensor_tensor(hidden[tpar][:], v_ps[tpar], bias[:, 1, t:t + 1], gated[tpar][:],
                                               ALU.add, ALU.mult).then_inc(v_used, 1)
                dve.wait_ge(v_used, T + 1)
                if routed:
                    par0 = (tpar - t) % 2
                    own = [n for n in range(HT_ROUTED) if (par0 + n) % 2 == tpar]
                    half = HT_ROUTED // 2
                    dve.wait_ge(c_all_loaded[tpar], 32 * (c * half) + 32 * (own.index(t) + 1))
                    nc.vector.tensor_tensor(hidden[tpar][:], hidden[tpar][:], c_all[tpar][:],
                                            ALU.mult).then_inc(hidden_done, 1)
                else:
                    settle(dve, passed_dve)
                    dve.engine_nop().then_inc(hidden_done, 1)

            def add_x1(c, f):
                dve.wait_ge(tr_full, 2 * c + (f + 1))
                dve.wait_ge(x1b_loaded, 16 * (c + 1))
                nc.vector.tensor_tensor(x1_b[:, 2 * f:2 * f + 2, :], tr_ps[f].rearrange("p (q d) -> p q d", q=2),
                                        x1_b[:, 2 * f:2 * f + 2, :], ALU.add).then_inc(y_sum, 1)
                dve.wait_ge(y_sum, 2 * c + (f + 1))
                layer_norm_stats(x1_b, f, ln2_step, 4 * c)

            def finish(c):
                dve.wait_ge(rstd2_step, 2 * c + 2)
                normalize(x1_b, y_done)

            def chunk(c, par):
                first = isinstance(c, int) and c == 0
                for t in range(HT):
                    if first and t + 2 < HT:
                        split_w(t + 2)
                    hide(c, HT * c + t, t, (par + t) % 2)
                    if not first and t in (4, 5):
                        add_x1(c - 1, t - 4)
                    if not first and t == 7:
                        finish(c - 1)
                    if first:
                        epilogue(t)

            dve.wait_ge(b2_step, 1)
            nc.vector.tensor_tensor(B2[1][:], b2_raw, B2[0][:].bitcast(fp32), ALU.subtract).then_inc(b2_step, 1)
            for n in range(2):
                last = nc.vector.memset(CT[n][2 * E:2 * E + 1, :].bitcast(fp32), 1.0)
            last.then_inc(b2_step, 1)
            chunk(0, 0)
            by_two(dve, chunk, 1, LAST - 1)
            chunk(LAST, LAST % 2)
            for f in range(2):
                add_x1(LAST, f)
            finish(LAST)

        @block.gpsimd
        def _(pool):
            def mask(G, kt):
                pool.wait_ge(exp_done, 8 * G + (2 * kt + 2))
                settle(pool, passed_pool)
                diag = probs[kt][:, :, 0:P]
                nc.gpsimd.affine_select(out=diag, in_=diag, pattern=[[0, GH], [1, P]], compare_op=ALU.is_ge,
                                        fill=0.0, base=0, channel_multiplier=-1).then_inc(mask_done, 1)

            def split_x(nb):
                pool.wait_ge(xT_hi_done, nb + 1)
                nc.gpsimd.tensor_tensor(XT[1][:], xT_raw[:], XT[0][:].bitcast(fp32), ALU.subtract).then_inc(
                    xT_lo_done, 1)

            def misc_stage(b, g, stage, n):
                t = b - 1
                if stage[0] in "tx":
                    k = int(stage[1])
                    pool.wait_ge(misc_free, n)
                    nc.gpsimd.tensor_tensor(t_lo[:, k, :], t_raw[:, k, :], t_hi[:, k, :].bitcast(fp32),
                                            ALU.subtract).then_inc(t_lo_done, 1)
                elif stage == "c":
                    pool.wait_ge(misc_free, n)
                    nc.gpsimd.tensor_tensor(cT_lo[:], cT_raw[:], cT_hi[:].bitcast(fp32), ALU.subtract).then_inc(
                        cT_lo_done, 1)

            def last_part(nb, tile):
                part, half = parts[tile // 2], tile % 2
                pool.wait_ge(part_m_done, 4 * nb + (tile + 1))
                nc.gpsimd.tensor_tensor(part[2][:, half, :], rest[:, half, :], part[1][:, half, :],
                                        ALU.subtract).then_inc(part_l_done, 1)

            def inverse_std(ready, step, c):
                pool.wait_ge(ready, 4 * c + 4)
                settle(pool, passed_pool)
                nc.gpsimd.tensor_scalar(var_eps[:], mean_var[:, :, 1], EPS, None, ALU.add).then_inc(step, 1)
                pool.wait_ge(step, 2 * c + 1)
                nc.gpsimd.tensor_tensor(rstd[:], var_eps[:], half_neg[:], ALU.pow).then_inc(step, 1)

            def iteration(b, par):
                whole = isinstance(b, int)
                for g in range(NG):
                    G = 4 * b + g
                    for s in range(SUBS):
                        if s % 2:
                            mask(G, s // 2)
                        stage = MISC.get((g, s))
                        if stage and has(b, g, stage):
                            misc_stage(b, g, stage, fill_no(b, (g, s)))
                        if (g, s) in PARTS_AT and not (whole and b == LAST):
                            last_part(b + 1, PARTS_AT[g, s])
                        if (g, s) == INVERSE_AT and not (whole and b == 0):
                            inverse_std(ln_step, rstd_step, b - 1)
                        if (g, s) == SPLIT_X_AT and not (whole and b == LAST):
                            split_x(b + 2)

            nc.gpsimd.memset(ident[:], 0.0).then_inc(cleared, 1)
            nc.gpsimd.memset(ident_bf[:], 0.0).then_inc(cleared, 1)
            nc.gpsimd.memset(causal[:], 0.0).then_inc(cleared, 1)
            nc.gpsimd.memset(half_neg[:], -0.5)
            for n in range(2):
                nc.gpsimd.memset(values[n][:, :, :, HD:32], 0.0).then_inc(cleared, 1)
            pool.wait_ge(cleared, 6)
            for m in (ident, ident_bf):
                nc.gpsimd.affine_select(out=m[:], in_=m[:], pattern=[[-1, P]], compare_op=ALU.not_equal, fill=1.0,
                                        base=0, channel_multiplier=1).then_inc(consts, 1)
            nc.gpsimd.affine_select(out=causal[:], in_=causal[:], pattern=[[-1, P]], compare_op=ALU.is_ge,
                                    fill=MASKED, base=0, channel_multiplier=1).then_inc(consts, 1)
            for n in range(2):
                nc.gpsimd.memset(values[n][:, :, :, HD:HD + 1], 1.0).then_inc(consts, 1)
            split_x(0)
            for tile in range(4):
                last_part(0, tile)
            split_x(1)
            iteration(0, 0)
            by_two(pool, iteration, 1, LAST - 1)
            iteration(LAST, LAST % 2)

            def epilogue(t):
                if t in EPILOGUE_AT:
                    misc_stage(B, 0, EPILOGUE_AT[t], FILLS_BEFORE_EPILOGUE + EPILOGUE.index(EPILOGUE_AT[t]) + 1)
                if t == INVERSE_TILE:
                    inverse_std(ln_step, rstd_step, LAST)

            def low(T, tpar):
                pool.wait_ge(h_hi_done, T + 1)
                nc.gpsimd.tensor_tensor(h_lo[tpar][:], hidden[tpar][:], h_hi[tpar][:].bitcast(fp32),
                                        ALU.subtract).then_inc(h_lo_done, 1)

            def chunk(c, par):
                first = isinstance(c, int) and c == 0
                for t in range(HT):
                    if first:
                        epilogue(t)
                    low(HT * c + t, (par + t) % 2)
                    if not first and t == 5:
                        inverse_std(ln2_step, rstd2_step, c - 1)

            chunk(0, 0)
            by_two(pool, chunk, 1, LAST - 1)
            chunk(LAST, LAST % 2)
            inverse_std(ln2_step, rstd2_step, LAST)




def laid_out(i):
    f = {k: np.asarray(v) for k, v in i.items()}
    x = f["L0_attn_x"]
    wqkv = f["L0_attn_w_qkv"].reshape(KD, P, 3, HEADS // 2, 2, HD)
    wqk = wqkv[:, :, 0:2].transpose(1, 0, 2, 4, 5, 3).reshape(P, KD * 4 * P)
    wv = f["L0_attn_w_qkv"].reshape(KD, P, 3, D)[:, :, 2].transpose(1, 0, 2).reshape(P, KD * D)
    hidden = HT * P

    def rows(routed, shared):
        a = np.zeros((hidden, routed.shape[-1]), routed.dtype)
        a[:E * H] = routed.reshape(E * H, -1)
        a[E * H:E * H + HS] = shared
        return a

    w1 = rows(f["L0_ffn_w1"], f["L0_ffn_ws1"])
    w3 = rows(f["L0_ffn_w3"], f["L0_ffn_ws3"])
    w2 = rows(f["L0_ffn_w2"].transpose(0, 2, 1), f["L0_ffn_ws2"].T)
    up = [w.reshape(HT, P, KD, P).transpose(0, 3, 2, 1) for w in (w1, w3)]
    wt = np.concatenate([*up, w2.reshape(HT, P, KD, P)], axis=2)
    b13 = np.stack([rows(f["L0_ffn_b1"].reshape(E, H, 1), f["L0_ffn_bs1"][:, None]),
                    rows(f["L0_ffn_b3"].reshape(E, H, 1), f["L0_ffn_bs3"][:, None])])
    b13 = b13.reshape(2, HT, P).transpose(2, 0, 1)
    b2 = np.concatenate([f["L0_ffn_b2"], f["L0_ffn_b2"], f["L0_ffn_bs2"][None]])
    return {
        "xT": np.concatenate([x, x[:1]]).reshape(B + 1, S, KD, P).transpose(0, 3, 2, 1),
        "x": x.reshape(B, QT, P, D).transpose(0, 2, 1, 3),
        "wqk": wqk,
        "wv": wv,
        "wo": f["L0_attn_w_out"].reshape(KD, P, D).transpose(1, 0, 2).reshape(P, KD * D),
        "gw": f["L0_ffn_gate_w"].T.reshape(KD, P, E).transpose(1, 0, 2),
        "gb": np.broadcast_to(f["L0_ffn_gate_b"], (P, E)),
        "wt": wt,
        "b13": b13,
        "b2": b2,
    }


def kernel(**inputs):
    import concourse.bacc as bacc
    from concourse.bass_utils import run_bass_kernel_spmd as run

    nc = bacc.Bacc("TRN2", target_bir_lowering=False, num_devices=1)
    arrays, args = {}, {}
    for name, a in laid_out(inputs).items():
        a = np.ascontiguousarray(a)
        arrays[f"in_{name}"] = a
        args[name] = nc.dram_tensor(f"in_{name}", a.shape, mybir.dt.from_np(a.dtype), kind="ExternalInput").ap()
    args["out"] = nc.dram_tensor("out_0", (B, P, QT, D), mybir.dt.float32, kind="ExternalOutput").ap()
    postln_layer(nc, **args)
    got = run(nc, [arrays], core_ids=[0]).results[0]["out_0"]
    return np.ascontiguousarray(got.transpose(0, 2, 1, 3)).reshape(B, S, D)
```

```python
from contextlib import ExitStack

import numpy as np

import concourse.bass as bass
from concourse import mybir

P = 128
B, S, D = 8, 512, 256
HEADS, HD = 16, 16
E, H, HS, TOP_K = 16, 176, 352, 6
KD = D // P
QT = S // P
GH = 4
NG = HEADS // GH
SUBS = 8
STACK = 6 * HD
SHIFT_ROWS = 3
Q_BLOCKS = (0, 0, 0, 1, 1, 2)
K_BLOCKS = (0, 1, 2, 0, 1, 0)
FILLS = 11
HT = -(-(E * H + HS) // P)
HT_ROUTED = E * H // P
BIAS_ROWS = 4 * E + 2
EPS = 1e-5
MASKED = -1e30
TAKEN = -3.0e38
TWO_ONES = float(np.array([0x3F803F80], np.uint32).view(np.float32)[0])
ABOVE_ALL = 3.3e38

PROB_FILLS = [(kt, (2 * pair + i,)) for kt in (0, 1) for pair in range(2) for i in range(2)] + [
    (kt, (2 * pair, 2 * pair + 1)) for kt in (2, 3) for pair in range(2)]
PROB_FILLS_OF_SUB = [(0, 1), (2, 3), (4, 5), (6, 7), (8,), (9,), (10,), (11,)]
SF = len(PROB_FILLS)
ST_BANKS = 3
assert SF % ST_BANKS == 0
SCORE_FILLS = (
    [(3, (h,)) for h in range(4)] + [(2, (h,)) for h in range(4)] + [(1, (0, 1)), (1, (2, 3)), (0, (0, 1, 2, 3))]
)
FILLS_OF_SUB = [
    [2, 1, 2, 2, 0, 2, 0, 2],
    [2, 1, 2, 1, 1, 2, 0, 2],
    [2, 1, 2, 1, 1, 2, 0, 2],
    [2, 1, 2, 1, 1, 2, 1, 1],
]

MISC = {
    (0, 0): "m", (0, 1): "q0", (0, 2): "q1", (0, 3): "v0", (0, 4): "k0", (0, 5): "k1", (0, 6): "v1", (0, 7): "t0",
    (1, 1): "t1", (1, 2): "m", (1, 4): "p0", (1, 5): "p1",
    (2, 1): "m", (2, 4): "x0", (2, 5): "x1",
    (3, 0): "m", (3, 1): "r", (3, 7): "c",
}
REST_AT = {(0, 1): 0, (0, 2): 1, (0, 4): 2, (0, 5): 3}
PARTS_AT = {(0, 2): 0, (0, 3): 1, (0, 5): 2, (0, 6): 3}
SUM_AT = {(1, 4): 0, (1, 6): 1}
STATS_AT = {(1, 5): 0, (1, 6): 1}
INVERSE_AT = (1, 7)
NORMALIZE_AT = {(2, 0): 0, (2, 1): 1}
ROUTE_AT = {(3, 1): 0, (3, 2): 1, (3, 4): 2, (3, 5): 3, (3, 6): 4}
SOFTMAX_AT = (3, 2)
SHIFT_AT = {(0, 3): 0, (0, 5): 1, (1, 3): 0, (1, 4): 1, (2, 2): 0, (2, 3): 1, (3, 1): 0, (3, 3): 1}
SPLIT_X_AT = (3, 1)
ATTEND_AT = {1: 1, 2: 2, 3: 3}
READ_AT, ROWS_AT, RECIP_AT, NORM_AT, ATTEND_FIRST_AT = 3, 5, 5, 6, 7
PE_ORDER = [
    ["FAPMG", "AFGPM", "FPMGA", "AFPMG", "FAPMG", "FPGAM", "AFGMP", "FPGAM"],
    ["FAPMG", "APFMG", "FPMGA", "FGPMA", "FPGMA", "FGAMP", "PFGMA", "FPGAM"],
    ["FAPMG", "PFAMG", "FPMGA", "PAMFG", "FAMPG", "FPGAM", "AFPMG", "FPGAM"],
    ["PAMFG", "APFMG", "FPMGA", "AFPMG", "FAMGP", "FPGAM", "FPAMG", "FPGAM"],
]
MAXIMA_AHEAD = [
    [1, 2, 2, 1, 2, 2, 0, 0],
    [1, 1, 2, 0, 2, 2, 0, 0],
    [1, 2, 2, 1, 1, 2, 0, 2],
    [1, 2, 2, 1, 1, 2, 0, 0],
]
PROBS_AHEAD = [
    [2, 2, 2, 2, 1, 2, 1, 2],
    [2, 2, 2, 2, 1, 2, 1, 2],
    [1, 2, 1, 2, 1, 2, 1, 2],
    [2, 0, 2, 0, 1, 2, 1, 2],
]
NEXT_BATCH = ("q0", "q1", "k0", "k1", "v0", "v1")
QK = NEXT_BATCH[:4]
BATCH_BEFORE = ("t0", "t1", "p0", "p1", "x0", "x1", "r", "c")
PROLOGUE = ["q0", "q1", "k0", "k1", "v0", "v1", "m"]
EPILOGUE = list(BATCH_BEFORE)
WARM_UP = 9
ROWS_TILE = 1
FIRST_W_AT = {(3, 4): 0, (3, 5): 1}
EPILOGUE_AT = {2: "t0", 3: "t1", 4: "p0", 5: "p1", 7: "x0", 8: "x1", 9: "r", 11: "c"}
INVERSE_TILE, NORMALIZE_TILE, SOFTMAX_TILE, STORE_X1_TILE, STORE_C_TILE = 5, 6, 10, 11, 12
W_AFTER_A = 16


def fills_of(g, s):
    done = sum(FILLS_OF_SUB[g][:s])
    return tuple(range(done, done + FILLS_OF_SUB[g][s]))


def key_of(stage, g=None):
    return [k for k in MISC if MISC[k] == stage and g in (None, k[0])][0]


def has(b, g, stage):
    first, last = isinstance(b, int) and b == 0, isinstance(b, int) and b == B - 1
    if first and stage in BATCH_BEFORE:
        return False
    return not (last and (stage in NEXT_BATCH or (stage == "m" and g == NG - 1)))


MISC_FIRST = [k for k in MISC if has(0, k[0], MISC[k])]


def fill_of(n, b=1):
    return n % 2, (b - 1) * (len(MISC) // 2) + (n + 1) // 2


def fill_no(b, key):
    if isinstance(b, int) and b == 0:
        return fill_of(len(PROLOGUE) + MISC_FIRST.index(key) + 1)
    keys = list(MISC)
    if isinstance(b, int) and b == B - 1:
        keys = [k for k in keys if has(b, k[0], MISC[k])]
    return fill_of(len(PROLOGUE) + len(MISC_FIRST) + keys.index(key) + 1, b)


FILLS_BEFORE_EPILOGUE = (
    len(PROLOGUE) + len(MISC_FIRST) + (B - 2) * len(MISC) + len([k for k in MISC if has(B - 1, k[0], MISC[k])])
)
assert len(MISC) % 2 == 0


def epilogue_fill(stage):
    return fill_of(FILLS_BEFORE_EPILOGUE + EPILOGUE.index(stage) + 1)


def postln_layer(nc, xT, x, wqk, wv, wo, gw, gb, wt, b13, b2, out):
    fp32, f32r, bf16 = mybir.dt.float32, mybir.dt.float32r, mybir.dt.bfloat16
    ALU, ACT, AX = mybir.AluOpType, mybir.ActivationFunctionType, mybir.AxisListType

    ctx = ExitStack()
    phase_a = ExitStack()

    def sem(name):
        return ctx.enter_context(nc.semaphore(name))

    def sb(name, shape, dt=fp32, where=ctx):
        return where.enter_context(nc.sbuf_tensor(name, shape, dt))

    def sa(name, shape, dt=fp32):
        return sb(name, shape, dt, phase_a)

    with ctx:
        x1_d = nc.dram_tensor("x1_d", (B, P, QT, D), fp32).ap()
        x1T_d = nc.dram_tensor("x1T_d", (B, 2, P, KD, S), fp32).ap()
        c_d = nc.dram_tensor("c_d", (3, E, B, S), fp32).ap()

        ident = sb("ident", [P, P])
        half_neg = sb("half_neg", [P, QT])
        stats = sb("stats", [P, QT, 6])
        mean_var = sb("mean_var", [P, QT, 2])
        var_eps = sb("var_eps", [P, QT])
        rstd = sb("rstd", [P, QT])

        stack_q, stack_k = [None, None], [None, None]
        stack_q[0] = sa("stack_q0", [P, HEADS, S], bf16)
        stack_k[0] = sa("stack_k0", [P, HEADS, S], bf16)
        parts = [[sa(f"{n}_{p}", [P, 2, S], bf16) for p in ("h", "m", "l")] for n in ("q", "k")]
        rest = sa("rest", [P, 2, S])
        xT_raw = sa("xT_raw", [P, KD, S])
        XT = [sa(f"xT_{n}", [P, KD, S], f32r) for n in ("hi", "lo")]
        WQK = [sa(f"wqk_{n}", [P, KD, 4, P], f32r) for n in ("hi", "lo")]
        WV = [sa(f"wv_{n}", [P, KD, D], f32r) for n in ("hi", "lo")]
        stack_q[1] = sa("stack_q1", [P, HEADS, S], bf16)
        stack_k[1] = sa("stack_k1", [P, HEADS, S], bf16)
        probs = [sa(f"probs{kt}", [P, GH, S - P * kt]) for kt in range(QT)]
        values = [sa(f"values{n}", [P, QT, HEADS, 32]) for n in range(2)]
        ident_bf = sa("ident_bf", [P, P], bf16)
        causal = sa("causal", [P, P], bf16)
        shift = sa("shift", [E, P])
        shift_rest = sa("shift_rest", [E, P])
        shift_parts = [[sa(f"shift_{p}{n}", [E, P], bf16) for p in ("h", "m", "l")] for n in range(2)]
        rowmax = [sa(f"rowmax{n}", [P, GH, QT]) for n in range(2)]
        attn_T = sa("attn_T", [P, S])
        attn = sa("attn", [P, QT, D])
        recip = sa("recip", [P, QT, GH])
        WO = [sa(f"wo_{n}", [P, KD, D], f32r) for n in ("hi", "lo")]
        GW = sa("gw_hi_lo", [P, KD, 2 * E], f32r)
        gw_raw = sa("gw_raw", [P, KD, E])
        gate_b = sa("gate_b", [P, E])
        x_res = sa("x_res", [P, QT, D])
        t_raw = sa("t_raw", [P, KD, S])
        t_hi = sa("t_hi", [P, KD, S], f32r)
        t_lo = sa("t_lo", [P, KD, S], f32r)
        x1 = sa("x1", [P, QT, D])
        logit_lo = sa("logit_lo", [P, QT, E])
        logits = sa("logits", [P, QT, E])
        top = sa("top", [P, QT])
        expo = sa("expo", [P, QT, E])
        total = sa("total", [P, QT])
        gate = sa("gate", [P, QT, E])
        biased = sa("biased", [P, QT, E + 2])
        top8 = sa("top8", [P, QT, 8])
        marked = sa("marked", [P, QT, E + 2])
        weight = sa("weight", [P, QT, E])
        cT_raw = sa("cT_raw", [E, S])
        cT_hi = sa("cT_hi", [E, S], f32r)
        cT_lo = sa("cT_lo", [E, S], f32r)
        raw0 = probs[0][:].rearrange("p h t -> p (h t)")
        wqk_raw, wv_raw, wo_raw = raw0[:, 0:1024], raw0[:, 1024:1536], raw0[:, 1536:2048]
        phase_a.close()

        w_raw = [sb(f"w_raw{n}", [P, 6, P]) for n in range(2)]
        X1T = [sb("x1T_0", [P, 2, KD, S], f32r)]
        CT = [sb(f"cT_{n}", [BIAS_ROWS, S], f32r) for n in range(2)]
        bias = sb("bias13", [P, 2, HT])
        B2 = sb("b2_parts", [BIAS_ROWS, D], f32r)
        c_all = [sb(f"c_all{n}", [P, S]) for n in range(2)]
        gated = [sb(f"gated{n}", [P, S]) for n in range(2)]
        hidden = [sb(f"hidden{n}", [P, S]) for n in range(2)]
        b2_raw = hidden[1][0:BIAS_ROWS, 0:D]
        h_hi = [sb(f"h_hi{n}", [P, S], f32r) for n in range(2)]
        h_lo = [sb(f"h_lo{n}", [P, S], f32r) for n in range(2)]
        w_all = sb("w_hi_lo", [P, HT, 2, 6, P], f32r)
        W = [w_all[:, :, n] for n in range(2)]
        X1T.append(sb("x1T_1", [P, 2, KD, S], f32r))
        x1_b = sb("x1_b", [P, QT, D])

        psum = ctx.enter_context(nc.psum_tensor("psum", [P, 8, S], fp32))
        st = [psum[:, n, :] for n in range(ST_BANKS)]
        sm = [psum[:, 4 + n, :] for n in range(2)]
        ov = psum[:, 6, :]
        shared = [psum[:, n, :] for n in (3, 7)]
        shared_late = [psum[:, n, :] for n in (6, 7)]
        PROLOGUE_BANKS = [psum[:, n, :] for n in (0, 1, 2, 3, 6, 7)]
        u_ps = [psum[:, n, :] for n in range(2)]
        v_ps = [psum[:, 2 + n, :] for n in range(2)]
        y_ps = [psum[:, 4 + 2 * n:6 + 2 * n, :] for n in range(2)]

        wqk_loaded = sem("wqk_loaded")
        w_loaded = sem("w_loaded")
        gw_loaded = sem("gw_loaded")
        xT_loaded = sem("xT_loaded")
        xres_loaded = sem("xres_loaded")
        cleared = sem("cleared")
        ones_set = sem("ones_set")
        consts = sem("consts")
        w_hi_done = sem("w_hi_done")
        w_lo_done = sem("w_lo_done")
        xT_hi_done = sem("xT_hi_done")
        xT_lo_done = sem("xT_lo_done")
        misc_full = [sem(f"misc_full{n}") for n in range(2)]
        misc_free = [sem(f"misc_free{n}") for n in range(2)]
        rest_done = sem("rest_done")
        part_m_done = sem("part_m_done")
        part_l_done = sem("part_l_done")
        stack_loaded = sem("stack_loaded")
        sm_full = sem("sm_full")
        sm_free = sem("sm_free")
        shift_step = sem("shift_step")
        shift_loaded = sem("shift_loaded")
        st_full = sem("st_full")
        exp_done = sem("exp_done")
        mask_done = sem("mask_done")
        pv_done = sem("pv_done")
        attn_T_done = sem("attn_T_done")
        rows_full = sem("rows_full")
        rows_used = sem("rows_used")
        recip_done = sem("recip_done")
        t_lo_done = sem("t_lo_done")
        ln_step = sem("ln_step")
        rstd_step = sem("rstd_step")
        x1_done = sem("x1_done")
        x1_stored = sem("x1_stored")
        tail_free = sem("tail_free")
        router_step = sem("router_step")
        router_exp = sem("router_exp")
        cT_lo_done = sem("cT_lo_done")
        c_stored = sem("c_stored")
        passed_dve = sem("passed_dve")
        passed_pool = sem("passed_pool")
        passed_sp = sem("passed_sp")
        wt_loaded = [sem(f"wt_loaded{n}") for n in range(2)]
        small_loaded = sem("small_loaded")
        b2_step = sem("b2_step")
        wt_hi = sem("wt_hi")
        wt_lo = sem("wt_lo")
        x1T_loaded = [sem(f"x1T_loaded{n}") for n in range(2)]
        x1b_loaded = sem("x1b_loaded")
        c_all_loaded = [sem(f"c_all_loaded{n}") for n in range(2)]
        u_full = sem("u_full")
        v_full = sem("v_full")
        gated_done = sem("gated_done")
        v_used = sem("v_used")
        hidden_done = sem("hidden_done")
        h_hi_done = sem("h_hi_done")
        h_lo_done = sem("h_lo_done")
        down_done = sem("down_done")
        y_sum = sem("y_sum")
        ln2_step = sem("ln2_step")
        rstd2_step = sem("rstd2_step")
        y_done = sem("y_done")
        out_stored = sem("out_stored")

        block = ctx.enter_context(nc.Block())
        PARTS3 = ((0, 0), (0, 1), (1, 0))
        LAST = B - 1
        STEPS_R = 10

        def settle(eng, passed):
            eng.sem_inc(passed, 1)

        def by_two(eng, body, first, second_last):
            with eng.Fori(0, (second_last - first + 1) // 2) as turn:
                for k in range(2):
                    body(2 * turn + (first + k), (first + k) % 2)

        @block.sync
        def _(sp):
            sp.dma_start(wqk_raw, wqk).then_inc(wqk_loaded, 16)
            sp.dma_start(xT_raw[:], xT[0]).then_inc(xT_loaded, 16)
            sp.dma_start(wv_raw, wv).then_inc(w_loaded, 16)
            sp.dma_start(wo_raw, wo).then_inc(w_loaded, 16)
            sp.dma_start(gw_raw[:], gw).then_inc(gw_loaded, 16)
            sp.dma_start(gate_b[:], gb).then_inc(gw_loaded, 16)

            def load_stack(nb, par):
                for n, (dst, blocks) in enumerate(((stack_q[par], Q_BLOCKS), (stack_k[par], K_BLOCKS))):
                    sp.wait_ge(part_l_done, 4 * nb + (2 * n + 2))
                    for j, part in enumerate(blocks):
                        sp.dma_start(dst[HD * j:HD * j + HD, :, :], parts[n][part][:]).then_inc(stack_loaded, 16)

            def load_shift(G, par, gpar, g):
                sp.wait_ge(shift_step, 3 * G + 3)
                for j in range(SHIFT_ROWS):
                    sp.dma_start(
                        stack_q[par][STACK + j:STACK + j + 1, GH * g:GH * g + GH, :], shift_parts[gpar][j][:]
                    ).then_inc(shift_loaded, 16)

            def iteration(b, par):
                last = isinstance(b, int) and b == LAST
                first = isinstance(b, int) and b == 0
                if not last:
                    sp.wait_ge(xT_lo_done, b + 2)
                    sp.dma_start(xT_raw[:], xT[b + 2]).then_inc(xT_loaded, 16)
                load_shift(4 * b + 1, par, 1, 1)
                if not last:
                    if not first:
                        sp.wait_ge(st_full, SF * NG * b)
                    load_stack(b + 1, 1 - par)
                load_shift(4 * b + 2, par, 0, 2)
                if not first:
                    sp.wait_ge(x1_done, 2 * b)
                sp.dma_start(x_res[:], x[b]).then_inc(xres_loaded, 16)
                load_shift(4 * b + 3, par, 1, 3)
                if last:
                    load_first_chunk()
                if not first:
                    store_x1(b - 1)
                if not last:
                    load_shift(4 * b + 4, 1 - par, 0, 0)
                if not first:
                    store_c(b - 1)
                    sp.wait_ge(x1_stored, 48 * b)
                    sp.wait_ge(c_stored, 48 * b)
                    sp.sem_inc(tail_free, 1)

            def store_x1(t):
                sp.wait_ge(t_lo_done, 4 * t + 4)
                sp.dma_start(x1_d[t], x1[:]).then_inc(x1_stored, 16)
                sp.dma_start(x1T_d[t, 0], t_hi[:].bitcast(fp32)).then_inc(x1_stored, 16)
                sp.dma_start(x1T_d[t, 1], t_lo[:].bitcast(fp32)).then_inc(x1_stored, 16)

            def store_c(t):
                sp.wait_ge(cT_lo_done, t + 1)
                sp.dma_start(c_d[0, :, t, :], cT_raw[:]).then_inc(c_stored, 16)
                sp.dma_start(c_d[1, :, t, :], cT_hi[:].bitcast(fp32)).then_inc(c_stored, 16)
                sp.dma_start(c_d[2, :, t, :], cT_lo[:].bitcast(fp32)).then_inc(c_stored, 16)

            def load_w(t):
                if t >= 2:
                    sp.wait_ge(wt_lo, t - 1)
                sp.dma_start(w_raw[t % 2][:], wt[t]).then_inc(wt_loaded[t % 2], 16)

            def load_chunk(c, par):
                sp.dma_start(X1T[par][:].bitcast(fp32), x1T_d[c].rearrange("n p k t -> p n k t")).then_inc(
                    x1T_loaded[par], 16)
                for j in range(2):
                    sp.dma_start(CT[par][2 * E * j:2 * E * j + 2 * E, :].bitcast(fp32), c_d[1:3, :, c, :]).then_inc(
                        x1T_loaded[par], 16)

            def load_c_all(T, c, t, tpar):
                if not (isinstance(T, int) and T < 2):
                    sp.wait_ge(hidden_done, T - 1)
                    settle(sp, passed_sp)
                first_e, last_e = t * P // H, (t * P + P - 1) // H
                edge = last_e * H - t * P if last_e > first_e else P // 2
                for e, lo, hi in ((first_e, 0, edge), (last_e, edge, P)):
                    sp.dma_start(c_all[tpar][lo:hi, :], c_d[0, e, c, :].partition_broadcast(hi - lo)).then_inc(
                        c_all_loaded[tpar], 16)

            def chunk(c, par):
                whole = isinstance(c, int)
                for t in range(HT_ROUTED):
                    if whole and c == 0 and t + 2 < HT:
                        load_w(t + 2)
                    load_c_all(HT * c + t, c, t, (par + t) % 2)
                    if whole and c == 0 and t == STORE_X1_TILE:
                        store_x1(LAST)
                    if whole and c == 0 and t == STORE_C_TILE:
                        store_c(LAST)
                    if t == 4 and not (whole and c == LAST):
                        if not (whole and c == 0):
                            sp.wait_ge(down_done, (HT + 1) * c)
                        load_chunk(c + 1, 1 - par)
                    if t == 9:
                        if not (whole and c == 0):
                            sp.wait_ge(y_done, c)
                            store_out(c - 1)
                            sp.wait_ge(out_stored, 16 * c)
                        sp.dma_start(x1_b[:], x1_d[c]).then_inc(x1b_loaded, 16)
                for t in range(HT_ROUTED, HT - 2):
                    if whole and c == 0:
                        load_w(t + 2)

            def store_out(c):
                sp.dma_start(out[c], x1_b[:]).then_inc(out_stored, 16)

            def load_first_chunk():
                sp.wait_ge(part_l_done, 4 * B)
                sp.wait_ge(stack_loaded, 192 * B)
                sp.wait_ge(xT_lo_done, B + 1)
                sp.wait_ge(st_full, SF * NG * LAST + 1)
                load_w(0)
                load_w(1)
                sp.dma_start(bias[:], b13).then_inc(small_loaded, 16)
                sp.dma_start(b2_raw, b2).then_inc(small_loaded, 16)
                load_chunk(0, 0)

            sp.sem_inc(tail_free, 1)
            for n, (dst, blocks) in enumerate(((stack_q[0], Q_BLOCKS), (stack_k[0], K_BLOCKS))):
                for bank in range(2):
                    sp.wait_ge(misc_free[bank], n + 1)
                for part, ready in enumerate((None, part_m_done, part_l_done)):
                    if ready:
                        sp.wait_ge(ready, 2 * n + 2)
                    for j in range(6):
                        if blocks[j] == part:
                            sp.dma_start(dst[HD * j:HD * j + HD, :, :], parts[n][part][:]).then_inc(
                                stack_loaded, 16)
            sp.wait_ge(xT_lo_done, 1)
            sp.dma_start(xT_raw[:], xT[1]).then_inc(xT_loaded, 16)
            load_shift(0, 0, 0, 0)
            iteration(0, 0)
            by_two(sp, iteration, 1, LAST - 1)
            iteration(LAST, LAST % 2)
            chunk(0, 0)
            sp.wait_ge(x1_stored, 48 * B)
            sp.wait_ge(c_stored, 48 * B)
            by_two(sp, chunk, 1, LAST - 1)
            chunk(LAST, LAST % 2)
            for f in range(2):
                sp.wait_ge(y_done, B + f)
                sp.dma_start(out[LAST, :, 2 * f:2 * f + 2], x1_b[:, 2 * f:2 * f + 2]).then_inc(out_stored, 16)
            sp.wait_ge(out_stored, 16 * (B + 1))

        @block.tensor
        def _(pe):
            def fill(no, banks=shared):
                bank, count = no
                pe.wait_ge(misc_free[bank], count - 1)
                return banks[bank], misc_full[bank]

            def three_pass(dst, lhs, rhs):
                n = 0
                for k in range(KD):
                    for a, b in PARTS3:
                        last = nc.tensor.matmul(dst, lhs(a, k), rhs(b, k), start=n == 0, stop=n == 3 * KD - 1)
                        n += 1
                return last

            def scores_for_max(G, par, g, f):
                n = FILLS * G + f
                bank = (g + f) % 2
                if not (isinstance(n, int) and n < 2):
                    pe.wait_ge(sm_free, n - 1)
                qt, heads = SCORE_FILLS[f]
                width = P * (qt + 1)
                for i, h in enumerate(heads):
                    head = GH * g + h
                    dst = sm[bank][:, i * width:(i + 1) * width]
                    nc.tensor.matmul(dst, stack_q[par][0:STACK, head, qt * P:qt * P + P],
                                     stack_k[par][0:STACK, head, 0:width], start=True, stop=False)
                    last = nc.tensor.matmul(dst[:, width - P:width], ident_bf[:], causal[:], start=False, stop=True)
                last.then_inc(sm_full, 1)

            def scores(G, par, g, s):
                for f in PROB_FILLS_OF_SUB[s]:
                    kt, heads = PROB_FILLS[f]
                    n = SF * G + f
                    if not (isinstance(n, int) and n < ST_BANKS):
                        pe.wait_ge(exp_done, n - (ST_BANKS - 1))
                    width = S - kt * P
                    for i, h in enumerate(heads):
                        head = GH * g + h
                        last = nc.tensor.matmul(st[f % ST_BANKS][:, i * width:(i + 1) * width],
                                                stack_k[par][0:STACK + SHIFT_ROWS, head, kt * P:kt * P + P],
                                                stack_q[par][0:STACK + SHIFT_ROWS, head, kt * P:S],
                                                start=True, stop=True)
                    last.then_inc(st_full, 1)

            def attend(G, par, g, kt):
                if kt == 0 and not (isinstance(G, int) and G == 0):
                    pe.wait_ge(rows_used, G)
                pe.wait_ge(mask_done, 4 * G + (kt + 1))
                for j in range(GH):
                    last = nc.tensor.matmul(ov[32 * j:32 * j + 32, kt * P:S], values[par][:, kt, GH * g + j, :],
                                            probs[kt][:, j, :], start=kt == 0, stop=kt == QT - 1,
                                            skip_group_check=True)
                last.then_inc(pv_done, 1)

            def project_qk(misc, full, nb, tile):
                if tile == 0:
                    pe.wait_ge(xT_lo_done, nb + 1)
                three_pass(misc, lambda a, k: WQK[a][:, k, tile, :], lambda b, k: XT[b][:, k, :]).then_inc(
                    full, 1)

            def project_v(misc, full, f):
                for j in range(2):
                    qt = 2 * f + j
                    last = three_pass(misc[:, j * D:j * D + D], lambda a, k: XT[a][:, k, qt * P:qt * P + P],
                                      lambda b, k: WV[b][:, k, :])
                last.then_inc(full, 1)

            def transpose_max(misc, full, G, gpar):
                pe.wait_ge(sm_free, FILLS * G + FILLS)
                nc.tensor.transpose(misc[0:E, 0:P], rowmax[gpar][:].rearrange("p h q -> p (h q)"), ident[:]).then_inc(
                    full, 1)

            def transpose_out(G):
                pe.wait_ge(attn_T_done, G + 1)
                for qt in range(QT):
                    last = nc.tensor.transpose(ov[:, qt * P:qt * P + P], attn_T[:, qt * P:qt * P + P], ident[:])
                last.then_inc(rows_full, 1)

            def transpose_rows(misc, full, src, k):
                for qt in range(QT):
                    last = nc.tensor.transpose(misc[:, qt * P:qt * P + P], src[:, qt, k * P:k * P + P], ident[:])
                last.then_inc(full, 1)

            def project_out(misc, full, t, f):
                pe.wait_ge(t_lo_done, 4 * t + 2)
                for j in range(2):
                    qt = 2 * f + j
                    last = three_pass(misc[:, j * D:j * D + D],
                                      lambda a, k: (t_hi, t_lo)[a][:, k, qt * P:qt * P + P],
                                      lambda b, k: WO[b][:, k, :])
                last.then_inc(full, 1)

            def route(misc, full, t):
                pe.wait_ge(t_lo_done, 4 * t + 4)
                for qt in range(QT):
                    dst = misc[:, 2 * E * qt:2 * E * qt + 2 * E]
                    for k in range(KD):
                        nc.tensor.matmul(dst, t_hi[:, k, qt * P:qt * P + P], GW[:, k, :], start=k == 0, stop=False)
                    for k in range(KD):
                        last = nc.tensor.matmul(dst[:, 0:E], t_lo[:, k, qt * P:qt * P + P], GW[:, k, 0:E],
                                                start=False, stop=k == KD - 1)
                last.then_inc(full, 1)

            def transpose_weights(misc, full, t):
                pe.wait_ge(router_step, STEPS_R * (t + 1))
                for qt in range(QT):
                    last = nc.tensor.transpose(misc[0:E, qt * P:qt * P + P], weight[:, qt, :], ident[:])
                last.then_inc(full, 1)

            def misc_stage(b, g, stage, bank):
                misc, full = bank
                if stage in QK:
                    project_qk(misc, full, b + 1, QK.index(stage))
                elif stage[0] == "v":
                    project_v(misc, full, int(stage[1]))
                elif stage == "m":
                    transpose_max(misc, full, 4 * b + (g + 1), (g + 1) % 2)
                elif stage[0] == "t":
                    if stage == "t0":
                        pe.wait_ge(rows_used, NG * b)
                    transpose_rows(misc, full, attn, int(stage[1]))
                elif stage[0] == "p":
                    project_out(misc, full, b - 1, int(stage[1]))
                elif stage[0] == "x":
                    if stage == "x0":
                        pe.wait_ge(x1_done, 2 * b)
                    transpose_rows(misc, full, x1, int(stage[1]))
                elif stage == "r":
                    route(misc, full, b - 1)
                else:
                    transpose_weights(misc, full, b - 1)

            def iteration(b, par):
                whole = isinstance(b, int)
                for g in range(NG):
                    G = 4 * b + g
                    pe.wait_ge(stack_loaded, 192 * (b + 1))
                    pe.wait_ge(shift_loaded, 48 * (G + 1))
                    for s in range(SUBS):
                        stage = MISC.get((g, s))
                        for step in PE_ORDER[g][s]:
                            if step == "P":
                                scores(G, par, g, s)
                            if step in "FG" and not (whole and 4 * b + g + 2 >= NG * B):
                                if g == 2 and s == 0 and step == "F":
                                    pe.wait_ge(stack_loaded, 192 * (b + 2))
                                for f in fills_of(g, s)[:1] if step == "F" else fills_of(g, s)[1:]:
                                    scores_for_max(G + 2, par if g < 2 else 1 - par, (g + 2) % NG, f)
                            if step == "A" and not (whole and b == 0 and g == 0):
                                if s in ATTEND_AT:
                                    attend(G - 1, par if g else 1 - par, (g - 1) % NG, ATTEND_AT[s])
                                if s == ROWS_AT:
                                    transpose_out(G - 1)
                            if step == "A" and s == ATTEND_FIRST_AT:
                                attend(G, par, g, 0)
                            if step == "M" and stage and has(b, g, stage):
                                misc_stage(b, g, stage, fill(fill_no(b, (g, s))))

            pe.wait_ge(consts, 5)
            for _ in range(WARM_UP):
                nc.tensor.matmul(ov[:, 0:P], ident[:], ident[:], start=True, stop=True)
            for n, stage in enumerate(PROLOGUE[:-1]):
                if stage in ("q0", "v0"):
                    pe.wait_ge(w_hi_done, 1 if stage == "q0" else 2)
                    pe.wait_ge(w_lo_done, 1 if stage == "q0" else 2)
                misc_stage(-1, 3, stage, (PROLOGUE_BANKS[n], misc_full[(n + 1) % 2]))
            pe.wait_ge(stack_loaded, 192)
            for G in range(2):
                for f in range(FILLS):
                    scores_for_max(G, 0, G, f)
                    if (G, f) == (1, 1):
                        for bank in range(2):
                            pe.wait_ge(misc_free[bank], 3)
                        transpose_max(*fill(fill_of(len(PROLOGUE))), 0, 0)
            pe.wait_ge(ones_set, 2)
            pe.wait_ge(w_lo_done, 4)
            iteration(0, 0)
            by_two(pe, iteration, 1, LAST - 1)
            iteration(LAST, LAST % 2)

            def epilogue(t):
                if t == 0:
                    for kt in (1, 2, 3):
                        attend(NG * B - 1, LAST % 2, NG - 1, kt)
                if t == ROWS_TILE:
                    transpose_out(NG * B - 1)
                if t in EPILOGUE_AT:
                    misc_stage(B, 0, EPILOGUE_AT[t], fill(epilogue_fill(EPILOGUE_AT[t]), shared_late))

            def up(T, t, par, tpar):
                for ps, full, used, first in ((u_ps, u_full, gated_done, 0), (v_ps, v_full, v_used, 2)):
                    if not (isinstance(T, int) and T < 2):
                        pe.wait_ge(used, T - 1)
                    three_pass(ps[tpar], lambda a, k: W[a][:, t, first + k, :],
                               lambda b, k: X1T[par][:, b, k, :]).then_inc(full, 1)

            def tokens(ps, qt):
                return ps[:, qt // 2, qt % 2 * D:qt % 2 * D + D]

            def down(T, t, par, tpar, halves=(range(QT),), last_of_chunk=False):
                pe.wait_ge(h_lo_done, T + 1)
                for tiles in halves:
                    for qt in tiles:
                        for n, (a, b) in enumerate(PARTS3):
                            last = nc.tensor.matmul(
                                tokens(y_ps[par], qt), (h_hi, h_lo)[a][tpar][:, qt * P:qt * P + P],
                                W[b][:, t, 4:6, :].rearrange("p d n -> p (d n)"),
                                start=t == 0 and n == 0 and qt % 2 == 0, stop=last_of_chunk and n == 2,
                                skip_group_check=True)
                    last.then_inc(down_done, 1)

            def down_bias(par, last_of_chunk=True):
                for qt in range(QT):
                    last = nc.tensor.matmul(tokens(y_ps[par], qt), CT[par][:, qt * P:qt * P + P], B2[:],
                                            start=False, stop=last_of_chunk, skip_group_check=True)
                last.then_inc(down_done, 1)

            def chunk(c, par):
                whole = isinstance(c, int)
                first = whole and c == 0
                for t in range(HT):
                    T = HT * c + t
                    if first:
                        pe.wait_ge(wt_hi, t + 1)
                        pe.wait_ge(wt_lo, t + 1)
                    if t == 0:
                        pe.wait_ge(x1T_loaded[par], (c + (2 - par)) * 24)
                    up(T, t, par, (par + t) % 2)
                    if t >= 2:
                        down(T - 2, t - 2, par, (par + t) % 2)
                    elif not first:
                        down(T - 2, HT - 2 + t, 1 - par, (par + t) % 2)
                        if t == 1:
                            pe.wait_ge(b2_step, 4)
                            down_bias(1 - par)
                    if first:
                        epilogue(t)

            for n in range(2):
                pe.wait_ge(misc_free[(FILLS_BEFORE_EPILOGUE - n) % 2], fill_of(FILLS_BEFORE_EPILOGUE - n)[1])
            pe.wait_ge(exp_done, SF * NG * B)
            chunk(0, 0)
            by_two(pe, chunk, 1, LAST - 1)
            chunk(LAST, LAST % 2)
            down_bias(LAST % 2, last_of_chunk=False)
            T = HT * B - 1
            down(T - 1, HT - 2, LAST % 2, (T - 1) % 2)
            down(T, HT - 1, LAST % 2, T % 2, (range(2), range(2, QT)), last_of_chunk=True)

        @block.scalar
        def _(act):
            def copy(dst, src, scale=1.0):
                return nc.scalar.activation(dst, src, ACT.Copy, scale=scale)

            def probabilities(G, fills):
                for f in fills:
                    kt, heads = PROB_FILLS[f]
                    n, width = len(heads), S - kt * P
                    act.wait_ge(st_full, SF * G + (f + 1))
                    if not (isinstance(G, int) and G == 0):
                        act.wait_ge(pv_done, 4 * G + (kt - 3))
                    nc.scalar.activation(probs[kt][:, heads[0]:heads[0] + n, :],
                                         st[f % ST_BANKS][:, 0:n * width].rearrange("p (h t) -> p h t", h=n),
                                         ACT.Exp).then_inc(exp_done, 1)

            def split_w(t):
                if t == W_AFTER_A:
                    act.wait_ge(x1_stored, 48 * B)
                    act.wait_ge(c_stored, 48 * B)
                act.wait_ge(wt_loaded[t % 2], 16 * (t // 2 + 1))
                copy(W[0][:, t], w_raw[t % 2][:]).then_inc(wt_hi, 1)

            def split_x(nb):
                act.wait_ge(xT_loaded, 16 * (nb + 1))
                copy(XT[0][:], xT_raw[:]).then_inc(xT_hi_done, 1)

            def transposed(misc, k):
                copy(t_hi[:, k, :], misc)
                return copy(t_raw[:, k, :], misc)

            def misc_stage(b, g, stage, no, misc=None):
                t = b - 1
                if stage in ("p0", "p1", "r"):
                    return
                bank, count = no
                act.wait_ge(misc_full[bank], count)
                if misc is None:
                    misc = shared[bank]
                if stage in QK:
                    tile = QK.index(stage)
                    scale = 0.25 if tile < 2 else 1.0
                    m = 4 * (b + 1) + tile
                    if tile == 0 and not (isinstance(b, int) and b == -1):
                        act.wait_ge(stack_loaded, 192 * (b + 1))
                    if not (isinstance(m, int) and m < 2):
                        act.wait_ge(part_l_done, m - 1)
                    copy(parts[tile // 2][0][:, tile % 2, :], misc, scale)
                    copy(rest[:, tile % 2, :], misc, scale).then_inc(misc_free[bank], 1)
                elif stage[0] == "v":
                    f = int(stage[1])
                    dst = values[(b + 1) % 2 if isinstance(b, int) else g][:, 2 * f:2 * f + 2, :, 0:HD]
                    copy(dst, misc.rearrange("p (q h d) -> p q h d", q=2, h=HEADS)).then_inc(misc_free[bank], 1)
                elif stage == "m":
                    G = 4 * b + (g + 1)
                    if not (isinstance(G, int) and G == 0):
                        act.wait_ge(shift_step, 3 * G)
                    if not (isinstance(G, int) and G < 2):
                        act.wait_ge(shift_loaded, 48 * (G - 1))
                    copy(shift_parts[(g + 1) % 2][0][:], misc[0:E, 0:P], -1.0)
                    copy(shift[:], misc[0:E, 0:P], -1.0).then_inc(misc_free[bank], 1)
                elif stage[0] == "t":
                    k = int(stage[1])
                    if k == 0:
                        act.wait_ge(tail_free, t + 1)
                    transposed(misc, k).then_inc(misc_free[bank], 1)
                elif stage[0] == "x":
                    k = int(stage[1])
                    act.wait_ge(t_lo_done, 4 * t + (k + 1))
                    transposed(misc, k).then_inc(misc_free[bank], 1)
                elif stage == "c":
                    copy(cT_hi[:], misc[0:E, :])
                    copy(cT_raw[:], misc[0:E, :]).then_inc(misc_free[bank], 1)

            def middle_part(nb, tile):
                act.wait_ge(rest_done, 4 * nb + (tile + 1))
                copy(parts[tile // 2][1][:, tile % 2, :], rest[:, tile % 2, :]).then_inc(part_m_done, 1)

            def read_attn(G):
                act.wait_ge(pv_done, 4 * G + 4)
                if not (isinstance(G, int) and G == 0):
                    act.wait_ge(recip_done, G)
                copy(attn_T[:], ov).then_inc(attn_T_done, 1)

            def router_softmax(t):
                act.wait_ge(router_step, STEPS_R * t + 3)
                nc.scalar.activation(expo[:], logits[:], ACT.Exp).then_inc(router_exp, 1)

            def iteration(b, par):
                whole = isinstance(b, int)
                for g in range(NG):
                    G = 4 * b + g
                    for s in range(SUBS):
                        probabilities(G, PROB_FILLS_OF_SUB[s][:PROBS_AHEAD[g][s]])
                        if s == READ_AT and not (whole and b == 0 and g == 0):
                            read_attn(G - 1)
                        stage = MISC.get((g, s))
                        if stage and has(b, g, stage):
                            misc_stage(b, 1 - par if stage[0] == "v" else g, stage, fill_no(b, (g, s)))
                        if (g, s) in PARTS_AT and not (whole and b == LAST):
                            middle_part(b + 1, PARTS_AT[g, s])
                        if (g, s) == SOFTMAX_AT and not (whole and b == 0):
                            router_softmax(b - 1)
                        if (g, s) == SPLIT_X_AT and not (whole and b == LAST):
                            split_x(b + 2)
                        if whole and b == LAST and (g, s) in FIRST_W_AT:
                            split_w(FIRST_W_AT[g, s])
                        probabilities(G, PROB_FILLS_OF_SUB[s][PROBS_AHEAD[g][s]:])

            act.wait_ge(wqk_loaded, 16)
            copy(WQK[0][:].rearrange("p k t m -> p (k t m)"), wqk_raw).then_inc(w_hi_done, 1)
            split_x(0)
            act.wait_ge(w_loaded, 32)
            copy(WV[0][:].rearrange("p k n -> p (k n)"), wv_raw).then_inc(w_hi_done, 1)
            copy(WO[0][:].rearrange("p k n -> p (k n)"), wo_raw).then_inc(w_hi_done, 1)
            act.wait_ge(gw_loaded, 32)
            copy(GW[:, :, 0:E], gw_raw[:]).then_inc(w_hi_done, 1)
            for n, stage in enumerate(PROLOGUE[:-1]):
                misc_stage(-1, 0, stage, fill_of(n + 1), PROLOGUE_BANKS[n])
            split_x(1)
            misc_stage(-1, 3, "m", fill_of(len(PROLOGUE)))
            act.wait_ge(w_lo_done, 4)
            iteration(0, 0)
            by_two(act, iteration, 1, LAST - 1)
            iteration(LAST, LAST % 2)

            def epilogue(t):
                if t == ROWS_TILE - 1:
                    read_attn(NG * B - 1)
                if t == SOFTMAX_TILE:
                    router_softmax(LAST)
                if t in EPILOGUE_AT:
                    no = epilogue_fill(EPILOGUE_AT[t])
                    misc_stage(B, 0, EPILOGUE_AT[t], no, shared_late[no[0]])

            def silu(T, t, tpar):
                act.wait_ge(u_full, T + 1)
                if not (isinstance(T, int) and T < 2):
                    act.wait_ge(v_used, T - 1)
                nc.scalar.activation(gated[tpar][:], u_ps[tpar], ACT.Silu, bias=bias[:, 0, t:t + 1]).then_inc(
                    gated_done, 1)

            def high(c, t, tpar):
                T = HT * c + t
                act.wait_ge(hidden_done, T + 1)
                if not (isinstance(T, int) and T < 2):
                    act.wait_ge(down_done, (HT + 1) * c + (t - 1 if t >= 2 else t - 2))
                copy(h_hi[tpar][:], hidden[tpar][:]).then_inc(h_hi_done, 1)

            def chunk(c, par):
                first = isinstance(c, int) and c == 0
                for t in range(HT):
                    if first and t + 2 < HT:
                        split_w(t + 2)
                    silu(HT * c + t, t, (par + t) % 2)
                    if not (first and t == 0):
                        high(c, t - 1, (par + t + 1) % 2)
                    if first:
                        epilogue(t)

            act.wait_ge(small_loaded, 32)
            copy(B2[:], b2_raw).then_inc(b2_step, 1)
            chunk(0, 0)
            by_two(act, chunk, 1, LAST - 1)
            chunk(LAST, LAST % 2)
            high(LAST, HT - 1, (LAST + HT - 1) % 2)

        @block.vector
        def _(dve):
            def split_w(t):
                dve.wait_ge(wt_hi, t + 1)
                nc.vector.tensor_tensor(W[1][:, t], w_raw[t % 2][:], W[0][:, t].bitcast(fp32),
                                        ALU.subtract).then_inc(wt_lo, 1)

            def maxima(G, g, f, gpar):
                qt, heads = SCORE_FILLS[f]
                width, n = P * (qt + 1), len(heads)
                dve.wait_ge(sm_full, FILLS * G + (f + 1))
                src = sm[(g + f) % 2][:, 0:n * width].rearrange("p (h k) -> p h k", h=n)
                nc.vector.reduce_max(rowmax[gpar][:, heads[0]:heads[0] + n, qt], src, AX.X).then_inc(
                    sm_free, 1)

            def layer_norm_stats(src, f, step, base):
                for qt in (2 * f, 2 * f + 1):
                    last = nc.vector.bn_stats(stats[:, qt, :], src[:, qt, :])
                last.then_inc(step, 1)
                dve.wait_ge(step, base + (2 * f + 1))
                settle(dve, passed_dve)
                for qt in (2 * f, 2 * f + 1):
                    last = nc.vector.bn_aggr(mean_var[:, qt, :], stats[:, qt, :])
                last.then_inc(step, 1)

            def normalize(buf, done, tiles=range(QT)):
                for qt in tiles:
                    last = nc.vector.tensor_scalar(buf[:, qt, :], buf[:, qt, :], mean_var[:, qt, 0:1],
                                                   rstd[:, qt:qt + 1], ALU.subtract, ALU.mult)
                last.then_inc(done, 1)

            def misc_stage(b, g, stage, no):
                t = b - 1
                if stage[0] == "p":
                    f = int(stage[1])
                    bank, count = no
                    dve.wait_ge(misc_full[bank], count)
                    if f == 0:
                        dve.wait_ge(xres_loaded, 16 * (t + 1))
                    nc.vector.tensor_tensor(x1[:, 2 * f:2 * f + 2, :],
                                            banks_of(b)[bank].rearrange("p (q d) -> p q d", q=2),
                                            x_res[:, 2 * f:2 * f + 2, :], ALU.add).then_inc(misc_free[bank], 1)

            def attn_stats(b, f, no):
                dve.wait_ge(misc_free[no[0]], no[1])
                layer_norm_stats(x1, f, ln_step, 4 * (b - 1))

            def banks_of(b):
                return shared_late if isinstance(b, int) and b == B else shared

            def rest_of(nb, tile, no):
                dve.wait_ge(misc_free[no[0]], no[1])
                nc.vector.tensor_tensor(rest[:, tile % 2, :], rest[:, tile % 2, :],
                                        parts[tile // 2][0][:, tile % 2, :], ALU.subtract).then_inc(rest_done, 1)

            def split_shift(G, gpar, no, step):
                high, mid, low = shift_parts[gpar]
                if step == 0:
                    dve.wait_ge(misc_free[no[0]], no[1])
                    nc.vector.tensor_tensor(shift_rest[:], shift[:], high[:], ALU.subtract).then_inc(shift_step, 1)
                elif step == 1:
                    dve.wait_ge(shift_step, 3 * G + 1)
                    nc.vector.tensor_copy(mid[:], shift_rest[:]).then_inc(shift_step, 1)
                else:
                    dve.wait_ge(shift_step, 3 * G + 2)
                    nc.vector.tensor_tensor(low[:], shift_rest[:], mid[:], ALU.subtract).then_inc(shift_step, 1)

            def rows_recip(G):
                dve.wait_ge(rows_full, G + 1)
                rows = ov.rearrange("p (q h c) -> p q h c", q=QT, h=GH)
                nc.vector.reciprocal(recip[:], rows[:, :, :, HD]).then_inc(recip_done, 1)

            def norm_rows(G, g):
                dve.wait_ge(recip_done, G + 1)
                rows = ov.rearrange("p (q h c) -> p q h c", q=QT, h=GH)
                dst = attn[:, :, g * GH * HD:(g + 1) * GH * HD]
                nc.vector.tensor_tensor(dst.rearrange("p q (h d) -> p q h d", h=GH), rows[:, :, :, 0:HD],
                                        recip[:].unsqueeze(3).to_broadcast([P, QT, GH, HD]),
                                        ALU.mult).then_inc(rows_used, 1)

            def route(t, no, part):
                base = STEPS_R * t
                if part == 0:
                    dve.wait_ge(misc_full[no[0]], no[1])
                    rows = banks_of(t + 1)[no[0]][:, 0:2 * E * QT].rearrange("p (q e) -> p q e", q=QT)
                    nc.vector.tensor_copy(logit_lo[:], rows[:, :, E:2 * E]).then_inc(router_step, 1)
                    dve.wait_ge(router_step, base + 1)
                    nc.vector.tensor_tensor(logits[:], rows[:, :, 0:E], logit_lo[:], ALU.add).then_inc(
                        misc_free[no[0]], 1)
                elif part == 1:
                    dve.wait_ge(misc_free[no[0]], no[1])
                    nc.vector.reduce_max(top[:], logits[:], AX.X).then_inc(router_step, 1)
                    dve.wait_ge(router_step, base + 2)
                    nc.vector.tensor_tensor(logits[:], logits[:], top[:].unsqueeze(2).to_broadcast([P, QT, E]),
                                            ALU.subtract).then_inc(router_step, 1)
                elif part == 2:
                    dve.wait_ge(router_exp, t + 1)
                    nc.vector.reduce_sum(total[:], expo[:], AX.X).then_inc(router_step, 1)
                    dve.wait_ge(router_step, base + 4)
                    nc.vector.reciprocal(total[:], total[:]).then_inc(router_step, 1)
                    dve.wait_ge(router_step, base + 5)
                    nc.vector.tensor_tensor(gate[:], expo[:], total[:].unsqueeze(2).to_broadcast([P, QT, E]),
                                            ALU.mult).then_inc(router_step, 1)
                elif part == 3:
                    dve.wait_ge(router_step, base + 6)
                    nc.vector.tensor_tensor(biased[:, :, 0:E], gate[:],
                                            gate_b[:].unsqueeze(1).to_broadcast([P, QT, E]),
                                            ALU.add).then_inc(router_step, 1)
                    dve.wait_ge(router_step, base + 7)
                    settle(dve, passed_dve)
                    for qt in range(QT):
                        last = nc.vector.max(top8[:, qt, :], biased[:, qt, :])
                    last.then_inc(router_step, 1)
                else:
                    dve.wait_ge(router_step, base + 8)
                    settle(dve, passed_dve)
                    for qt in range(QT):
                        last = nc.vector.match_replace(marked[:, qt, :], top8[:, qt, :], biased[:, qt, :], TAKEN)
                    last.then_inc(router_step, 1)
                    dve.wait_ge(router_step, base + 9)
                    nc.vector.scalar_tensor_tensor(weight[:], marked[:, :, 0:E], TAKEN, gate[:], ALU.is_equal,
                                                   ALU.mult).then_inc(router_step, 1)

            def iteration(b, par):
                whole = isinstance(b, int)
                for g in range(NG):
                    G = 4 * b + g
                    for s in range(SUBS):
                        shifts = has(b, g, "m") and (g, s) in SHIFT_AT
                        first_group = whole and b == 0 and g == 0
                        maxima_fills = () if whole and 4 * b + g + 2 >= NG * B else fills_of(g, s)
                        if shifts:
                            split_shift(G + 1, (g + 1) % 2, fill_no(b, key_of("m", g)), 2 * SHIFT_AT[g, s])
                        if s == NORM_AT and not first_group:
                            norm_rows(G - 1, (g - 1) % NG)
                        for f in maxima_fills[:MAXIMA_AHEAD[g][s]]:
                            maxima(G + 2, (g + 2) % NG, f, g % 2)
                        if shifts and SHIFT_AT[g, s] == 0:
                            split_shift(G + 1, (g + 1) % 2, fill_no(b, key_of("m", g)), 1)
                        if s == RECIP_AT and not first_group:
                            rows_recip(G - 1)
                        if not (whole and b == 0):
                            if (g, s) in SUM_AT:
                                stage = f"p{SUM_AT[g, s]}"
                                misc_stage(b, g, stage, fill_no(b, key_of(stage)))
                            if (g, s) in STATS_AT:
                                f = STATS_AT[g, s]
                                attn_stats(b, f, fill_no(b, key_of(f"p{f}")))
                            if (g, s) in NORMALIZE_AT:
                                f = NORMALIZE_AT[g, s]
                                dve.wait_ge(rstd_step, 2 * b)
                                normalize(x1, x1_done, (2 * f, 2 * f + 1))
                            if (g, s) in ROUTE_AT:
                                route(b - 1, fill_no(b, key_of("r")), ROUTE_AT[g, s])
                        if whole and b == LAST and (g, s) in FIRST_W_AT:
                            split_w(FIRST_W_AT[g, s])
                        for f in maxima_fills[MAXIMA_AHEAD[g][s]:]:
                            maxima(G + 2, (g + 2) % NG, f, g % 2)

            def epilogue(t):
                if t == ROWS_TILE:
                    rows_recip(NG * B - 1)
                    norm_rows(NG * B - 1, NG - 1)
                stage = EPILOGUE_AT.get(t)
                no = epilogue_fill(stage) if stage else None
                if stage in ("p0", "p1"):
                    misc_stage(B, 0, stage, no)
                    attn_stats(B, int(stage[1]), no)
                if t == NORMALIZE_TILE:
                    dve.wait_ge(rstd_step, 2 * B)
                    for f in range(2):
                        normalize(x1, x1_done, (2 * f, 2 * f + 1))
                if stage == "r":
                    for part in range(2):
                        route(LAST, no, part)
                if t == SOFTMAX_TILE:
                    for part in range(2, 5):
                        route(LAST, no, part)

            def ones(n):
                rows = stack_k[n][STACK:STACK + SHIFT_ROWS, :, :].rearrange("p h t -> p (h t)").bitcast(fp32)
                nc.vector.memset(rows, TWO_ONES).then_inc(ones_set, 1)

            nc.vector.memset(biased[:, :, E:E + 2], ABOVE_ALL).then_inc(cleared, 1)
            ones(0)
            for n, ((hi, lo), raw, names) in enumerate(
                    ((WQK, wqk_raw, "p k t m -> p (k t m)"), (WV, wv_raw, "p k n -> p (k n)"),
                     (WO, wo_raw, "p k n -> p (k n)"))):
                dve.wait_ge(w_hi_done, n + 1)
                nc.vector.tensor_tensor(lo[:].rearrange(names), raw, hi[:].bitcast(fp32).rearrange(names),
                                        ALU.subtract).then_inc(w_lo_done, 1)
                if n == 0:
                    dve.wait_ge(xT_hi_done, 1)
                    nc.vector.tensor_tensor(XT[1][:], xT_raw[:], XT[0][:].bitcast(fp32), ALU.subtract).then_inc(
                        xT_lo_done, 1)
            dve.wait_ge(w_hi_done, 4)
            nc.vector.tensor_tensor(GW[:, :, E:2 * E], gw_raw[:], GW[:, :, 0:E].bitcast(fp32),
                                    ALU.subtract).then_inc(w_lo_done, 1)
            for tile in range(4):
                rest_of(0, tile, fill_of(tile + 1))
                dve.wait_ge(rest_done, tile + 1)
                nc.vector.tensor_copy(parts[tile // 2][1][:, tile % 2, :], rest[:, tile % 2, :]).then_inc(
                    part_m_done, 1)
            ones(1)
            for G in range(2):
                for f in range(FILLS):
                    maxima(G, G, f, G)
                    if G == 1 and f in (2, 3, 4):
                        split_shift(0, 0, fill_of(len(PROLOGUE)), f - 2)
            iteration(0, 0)
            by_two(dve, iteration, 1, LAST - 1)
            iteration(LAST, LAST % 2)

            def hide(c, T, t, tpar):
                dve.wait_ge(gated_done, T + 1)
                dve.wait_ge(v_full, T + 1)
                if not (isinstance(T, int) and T < 2):
                    dve.wait_ge(h_lo_done, T - 1)
                routed = t < HT_ROUTED
                nc.vector.scalar_tensor_tensor(hidden[tpar][:], v_ps[tpar], bias[:, 1, t:t + 1], gated[tpar][:],
                                               ALU.add, ALU.mult).then_inc(v_used, 1)
                dve.wait_ge(v_used, T + 1)
                if routed:
                    par0 = (tpar - t) % 2
                    own = [n for n in range(HT_ROUTED) if (par0 + n) % 2 == tpar]
                    half = HT_ROUTED // 2
                    dve.wait_ge(c_all_loaded[tpar], 32 * (c * half) + 32 * (own.index(t) + 1))
                    nc.vector.tensor_tensor(hidden[tpar][:], hidden[tpar][:], c_all[tpar][:],
                                            ALU.mult).then_inc(hidden_done, 1)
                else:
                    settle(dve, passed_dve)
                    dve.engine_nop().then_inc(hidden_done, 1)

            def add_x1(c, f, par, done=None):
                dve.wait_ge(down_done, done or (HT + 1) * (c + 1))
                dve.wait_ge(x1b_loaded, 16 * (c + 1))
                nc.vector.tensor_tensor(x1_b[:, 2 * f:2 * f + 2, :],
                                        y_ps[par][:, f, :].rearrange("p (q d) -> p q d", q=2),
                                        x1_b[:, 2 * f:2 * f + 2, :], ALU.add).then_inc(y_sum, 1)
                dve.wait_ge(y_sum, 2 * c + (f + 1))
                layer_norm_stats(x1_b, f, ln2_step, 4 * c)

            def finish(c):
                dve.wait_ge(rstd2_step, 2 * c + 2)
                normalize(x1_b, y_done)

            def chunk(c, par):
                first = isinstance(c, int) and c == 0
                for t in range(HT):
                    if first and t + 2 < HT:
                        split_w(t + 2)
                    hide(c, HT * c + t, t, (par + t) % 2)
                    if not first and t in (4, 5):
                        add_x1(c - 1, t - 4, 1 - par)
                    if not first and t == 7:
                        finish(c - 1)
                    if first:
                        epilogue(t)

            dve.wait_ge(b2_step, 1)
            low_rows, shared_rows = slice(2 * E, 4 * E), slice(4 * E, BIAS_ROWS)
            nc.vector.tensor_tensor(B2[low_rows, :], b2_raw[low_rows], B2[low_rows, :].bitcast(fp32),
                                    ALU.subtract).then_inc(b2_step, 1)
            nc.vector.scalar_tensor_tensor(B2[shared_rows, :], B2[shared_rows, :].bitcast(fp32),
                                           ident[shared_rows, BIAS_ROWS - 1:BIAS_ROWS], b2_raw[shared_rows],
                                           ALU.mult, ALU.subtract).then_inc(b2_step, 1)
            for n in range(2):
                last = nc.vector.memset(CT[n][shared_rows, :].bitcast(fp32), -1.0)
            last.then_inc(b2_step, 1)
            chunk(0, 0)
            by_two(dve, chunk, 1, LAST - 1)
            chunk(LAST, LAST % 2)
            for f in range(2):
                add_x1(LAST, f, LAST % 2, (HT + 1) * B + f)
            for f in range(2):
                dve.wait_ge(rstd2_step, 2 * LAST + 2 * f + 2)
                normalize(x1_b, y_done, (2 * f, 2 * f + 1))

        @block.gpsimd
        def _(pool):
            def mask(G, kt):
                pool.wait_ge(exp_done, SF * G + (4, 8, 10, 12)[kt])
                settle(pool, passed_pool)
                diag = probs[kt][:, :, 0:P]
                nc.gpsimd.affine_select(out=diag, in_=diag, pattern=[[0, GH], [1, P]], compare_op=ALU.is_ge,
                                        fill=0.0, base=0, channel_multiplier=-1).then_inc(mask_done, 1)

            def split_x(nb):
                pool.wait_ge(xT_hi_done, nb + 1)
                nc.gpsimd.tensor_tensor(XT[1][:], xT_raw[:], XT[0][:].bitcast(fp32), ALU.subtract).then_inc(
                    xT_lo_done, 1)

            def misc_stage(b, g, stage, no):
                t = b - 1
                if stage[0] in "tx":
                    k = int(stage[1])
                    pool.wait_ge(misc_free[no[0]], no[1])
                    nc.gpsimd.tensor_tensor(t_lo[:, k, :], t_raw[:, k, :], t_hi[:, k, :].bitcast(fp32),
                                            ALU.subtract).then_inc(t_lo_done, 1)
                elif stage == "c":
                    pool.wait_ge(misc_free[no[0]], no[1])
                    nc.gpsimd.tensor_tensor(cT_lo[:], cT_raw[:], cT_hi[:].bitcast(fp32), ALU.subtract).then_inc(
                        cT_lo_done, 1)

            def rest_of(nb, tile, no):
                pool.wait_ge(misc_free[no[0]], no[1])
                nc.gpsimd.tensor_tensor(rest[:, tile % 2, :], rest[:, tile % 2, :],
                                        parts[tile // 2][0][:, tile % 2, :], ALU.subtract).then_inc(rest_done, 1)

            def last_part(nb, tile):
                part, half = parts[tile // 2], tile % 2
                pool.wait_ge(part_m_done, 4 * nb + (tile + 1))
                nc.gpsimd.tensor_tensor(part[2][:, half, :], rest[:, half, :], part[1][:, half, :],
                                        ALU.subtract).then_inc(part_l_done, 1)

            def inverse_std(ready, step, c, half=None):
                tiles = slice(0, QT) if half is None else slice(2 * half, 2 * half + 2)
                pool.wait_ge(ready, 4 * c + (4 if half is None else 2 * half + 2))
                settle(pool, passed_pool)
                nc.gpsimd.tensor_scalar(var_eps[:, tiles], mean_var[:, tiles, 1], EPS, None, ALU.add).then_inc(
                    step, 1)
                pool.wait_ge(step, 2 * c + (2 * (half or 0) + 1))
                nc.gpsimd.tensor_tensor(rstd[:, tiles], var_eps[:, tiles], half_neg[:, tiles], ALU.pow).then_inc(
                    step, 1)

            def iteration(b, par):
                whole = isinstance(b, int)
                for g in range(NG):
                    G = 4 * b + g
                    for s in range(SUBS):
                        if s % 2:
                            mask(G, s // 2)
                        stage = MISC.get((g, s))
                        if stage and has(b, g, stage):
                            misc_stage(b, g, stage, fill_no(b, (g, s)))
                        if (g, s) in REST_AT and not (whole and b == LAST):
                            tile = REST_AT[g, s]
                            rest_of(b + 1, tile, fill_no(b, key_of(QK[tile])))
                        if (g, s) in PARTS_AT and not (whole and b == LAST):
                            last_part(b + 1, PARTS_AT[g, s])
                        if (g, s) == INVERSE_AT and not (whole and b == 0):
                            inverse_std(ln_step, rstd_step, b - 1)
                        if (g, s) == SPLIT_X_AT and not (whole and b == LAST):
                            split_x(b + 2)

            nc.gpsimd.memset(ident[:], 0.0).then_inc(cleared, 1)
            nc.gpsimd.memset(ident_bf[:], 0.0).then_inc(cleared, 1)
            nc.gpsimd.memset(causal[:], 0.0).then_inc(cleared, 1)
            nc.gpsimd.memset(half_neg[:], -0.5)
            for n in range(2):
                nc.gpsimd.memset(values[n][:, :, :, HD:32], 0.0).then_inc(cleared, 1)
            pool.wait_ge(cleared, 6)
            for m in (ident, ident_bf):
                nc.gpsimd.affine_select(out=m[:], in_=m[:], pattern=[[-1, P]], compare_op=ALU.not_equal, fill=1.0,
                                        base=0, channel_multiplier=1).then_inc(consts, 1)
            nc.gpsimd.affine_select(out=causal[:], in_=causal[:], pattern=[[-1, P]], compare_op=ALU.is_ge,
                                    fill=MASKED, base=0, channel_multiplier=1).then_inc(consts, 1)
            for n in range(2):
                nc.gpsimd.memset(values[n][:, :, :, HD:HD + 1], 1.0).then_inc(consts, 1)
            for tile in range(4):
                last_part(0, tile)
            split_x(1)
            iteration(0, 0)
            by_two(pool, iteration, 1, LAST - 1)
            iteration(LAST, LAST % 2)

            def epilogue(t):
                if t in EPILOGUE_AT:
                    misc_stage(B, 0, EPILOGUE_AT[t], epilogue_fill(EPILOGUE_AT[t]))
                if t == INVERSE_TILE:
                    inverse_std(ln_step, rstd_step, LAST)

            def low(T, tpar):
                pool.wait_ge(h_hi_done, T + 1)
                nc.gpsimd.tensor_tensor(h_lo[tpar][:], hidden[tpar][:], h_hi[tpar][:].bitcast(fp32),
                                        ALU.subtract).then_inc(h_lo_done, 1)

            def chunk(c, par):
                first = isinstance(c, int) and c == 0
                for t in range(HT):
                    if first:
                        epilogue(t)
                    low(HT * c + t, (par + t) % 2)
                    if not first and t == 5:
                        inverse_std(ln2_step, rstd2_step, c - 1)

            chunk(0, 0)
            by_two(pool, chunk, 1, LAST - 1)
            chunk(LAST, LAST % 2)
            for half in range(2):
                inverse_std(ln2_step, rstd2_step, LAST, half)




def laid_out(i):
    f = {k: np.asarray(v) for k, v in i.items()}
    x = f["L0_attn_x"]
    wqkv = f["L0_attn_w_qkv"].reshape(KD, P, 3, HEADS // 2, 2, HD)
    wqk = wqkv[:, :, 0:2].transpose(1, 0, 2, 4, 5, 3).reshape(P, KD * 4 * P)
    wv = f["L0_attn_w_qkv"].reshape(KD, P, 3, D)[:, :, 2].transpose(1, 0, 2).reshape(P, KD * D)
    hidden = HT * P

    def rows(routed, shared):
        a = np.zeros((hidden, routed.shape[-1]), routed.dtype)
        a[:E * H] = routed.reshape(E * H, -1)
        a[E * H:E * H + HS] = shared
        return a

    w1 = rows(f["L0_ffn_w1"], f["L0_ffn_ws1"])
    w3 = rows(f["L0_ffn_w3"], f["L0_ffn_ws3"])
    w2 = rows(f["L0_ffn_w2"].transpose(0, 2, 1), f["L0_ffn_ws2"].T)
    up = [w.reshape(HT, P, KD, P).transpose(0, 3, 2, 1) for w in (w1, w3)]
    wt = np.concatenate([*up, w2.reshape(HT, P, KD, P)], axis=2)
    b13 = np.stack([rows(f["L0_ffn_b1"].reshape(E, H, 1), f["L0_ffn_bs1"][:, None]),
                    rows(f["L0_ffn_b3"].reshape(E, H, 1), f["L0_ffn_bs3"][:, None])])
    b13 = b13.reshape(2, HT, P).transpose(2, 0, 1)
    b2 = np.concatenate([f["L0_ffn_b2"]] * 4 + [f["L0_ffn_bs2"][None]] * 2)
    return {
        "xT": np.concatenate([x, x[:1]]).reshape(B + 1, S, KD, P).transpose(0, 3, 2, 1),
        "x": x.reshape(B, QT, P, D).transpose(0, 2, 1, 3),
        "wqk": wqk,
        "wv": wv,
        "wo": f["L0_attn_w_out"].reshape(KD, P, D).transpose(1, 0, 2).reshape(P, KD * D),
        "gw": f["L0_ffn_gate_w"].T.reshape(KD, P, E).transpose(1, 0, 2),
        "gb": np.broadcast_to(f["L0_ffn_gate_b"], (P, E)),
        "wt": wt,
        "b13": b13,
        "b2": b2,
    }


def kernel(**inputs):
    import concourse.bacc as bacc
    from concourse.bass_utils import run_bass_kernel_spmd as run

    nc = bacc.Bacc("TRN2", target_bir_lowering=False, num_devices=1)
    arrays, args = {}, {}
    for name, a in laid_out(inputs).items():
        a = np.ascontiguousarray(a)
        arrays[f"in_{name}"] = a
        args[name] = nc.dram_tensor(f"in_{name}", a.shape, mybir.dt.from_np(a.dtype), kind="ExternalInput").ap()
    args["out"] = nc.dram_tensor("out_0", (B, P, QT, D), mybir.dt.float32, kind="ExternalOutput").ap()
    postln_layer(nc, **args)
    got = run(nc, [arrays], core_ids=[0]).results[0]["out_0"]
    return np.ascontiguousarray(got.transpose(0, 2, 1, 3)).reshape(B, S, D)
```
